# Optimizing a Trainium2 kernel written in Bass

```python
import numpy as np
import jax
import jax.numpy as jnp

def _softmax(x, axis=-1):
    return jax.nn.softmax(x, axis=axis)

def _gelu(x):
    return jax.nn.gelu(x, approximate=True)

def _silu(x):
    return jax.nn.silu(x)

def _sigmoid(x):
    return jax.nn.sigmoid(x)

def _layernorm(x, axis=-1, eps=1e-05):
    m = jnp.mean(x, axis=axis, keepdims=True)
    v = jnp.var(x, axis=axis, keepdims=True)
    return (x - m) / jnp.sqrt(v + eps)

def _scatter_add(tgt, idx, src, axis=0):
    return tgt.at[idx].add(src)

def _segment_sum(src, seg, n):
    return jax.ops.segment_sum(src, seg, n)
kernel_name = 'mk_prb_d1_jaxref_r4_58ec1c'

def setup_inputs(seed: int=0):
    np.random.seed(seed)
    _w = jnp.asarray

    def _L0_attn_setup():
        import jax, jax.numpy as jnp
        import numpy as np
        NUM_HEADS = 16
        D_MODEL = 256
        HEAD_DIM = D_MODEL // NUM_HEADS
        EPS = 1e-06

        def _feature_map(x):
            return jax.nn.elu(x) + 1.0
        key = jax.random.key(seed)
        ks = jax.random.split(key, 9)
        B, S, D = (4, 2048, D_MODEL)
        scale = 1.0 / np.sqrt(D)
        inputs_q = jax.random.normal(ks[0], (B, S, D), dtype=jnp.float32)
        Wq = jax.random.normal(ks[1], (D, D), dtype=jnp.float32) * scale
        Wk = jax.random.normal(ks[2], (D, D), dtype=jnp.float32) * scale
        Wv = jax.random.normal(ks[3], (D, D), dtype=jnp.float32) * scale
        Wo = jax.random.normal(ks[4], (D, D), dtype=jnp.float32) * scale
        bq = jnp.zeros((D,), jnp.float32)
        bk = jnp.zeros((D,), jnp.float32)
        bv = jnp.zeros((D,), jnp.float32)
        bo = jnp.zeros((D,), jnp.float32)
        return {'inputs_q': inputs_q, 'Wq': Wq, 'bq': bq, 'Wk': Wk, 'bk': bk, 'Wv': Wv, 'bv': bv, 'Wo': Wo, 'bo': bo}
    _L0_attn_in = _L0_attn_setup()

    def _L0_ffn_setup():
        import jax, jax.numpy as jnp
        import numpy as np
        MODEL_DIM = 256
        HIDDEN = 512
        NUM_GROUPS = 2
        EXPERTS_PER_GP = 4
        NUM_EXPERTS = NUM_GROUPS * EXPERTS_PER_GP
        TOP_K = 2
        B, T = (2, 512)

        def _swiglu(x):
            a, b = jnp.split(x, 2, axis=-1)
            return jax.nn.silu(a) * b
        key = jax.random.key(seed)
        ks = jax.random.split(key, 7)
        s = 0.02
        return {'x': jax.random.normal(ks[0], (B, T, MODEL_DIM), jnp.float32), 'w_in': jax.random.normal(ks[1], (HIDDEN * 2, MODEL_DIM), jnp.float32) * s, 'w_out': jax.random.normal(ks[2], (MODEL_DIM, HIDDEN), jnp.float32) * s, 'w1': jax.random.normal(ks[3], (HIDDEN * 2, MODEL_DIM), jnp.float32) * s, 'w2': jax.random.normal(ks[4], (NUM_EXPERTS, MODEL_DIM, HIDDEN), jnp.float32) * s, 'wg': jax.random.normal(ks[5], (NUM_GROUPS, MODEL_DIM), jnp.float32) * s, 'we': jax.random.normal(ks[6], (NUM_EXPERTS, MODEL_DIM), jnp.float32) * s, 'gb': jnp.zeros((NUM_GROUPS,), jnp.float32), 'eb': jnp.zeros((NUM_EXPERTS,), jnp.float32)}
    _L0_ffn_in = _L0_ffn_setup()
    _d = {'L0_attn_inputs_q': _L0_attn_in['inputs_q'], 'L0_attn_Wq': _L0_attn_in['Wq'], 'L0_attn_bq': _L0_attn_in['bq'], 'L0_attn_Wk': _L0_attn_in['Wk'], 'L0_attn_bk': _L0_attn_in['bk'], 'L0_attn_Wv': _L0_attn_in['Wv'], 'L0_attn_bv': _L0_attn_in['bv'], 'L0_attn_Wo': _L0_attn_in['Wo'], 'L0_attn_bo': _L0_attn_in['bo'], 'L0_ffn_w_in': _L0_ffn_in['w_in'], 'L0_ffn_w_out': _L0_ffn_in['w_out'], 'L0_ffn_w1': _L0_ffn_in['w1'], 'L0_ffn_w2': _L0_ffn_in['w2'], 'L0_ffn_wg': _L0_ffn_in['wg'], 'L0_ffn_we': _L0_ffn_in['we'], 'L0_ffn_gb': _L0_ffn_in['gb'], 'L0_ffn_eb': _L0_ffn_in['eb']}
    _x0 = _d['L0_attn_inputs_q']
    _d['L0_attn_inputs_q'] = jax.random.normal(jax.random.fold_in(jax.random.key(seed), 1), (16, 512, 256), dtype=_x0.dtype)
    del _x0
    return _d

def reference(L0_attn_inputs_q, L0_attn_Wq, L0_attn_bq, L0_attn_Wk, L0_attn_bk, L0_attn_Wv, L0_attn_bv, L0_attn_Wo, L0_attn_bo, L0_ffn_w_in, L0_ffn_w_out, L0_ffn_w1, L0_ffn_w2, L0_ffn_wg, L0_ffn_we, L0_ffn_gb, L0_ffn_eb):

    def _L0_attn_ref(inputs_q, Wq, bq, Wk, bk, Wv, bv, Wo, bo):
        import jax, jax.numpy as jnp
        import numpy as np
        NUM_HEADS = 16
        D_MODEL = 256
        HEAD_DIM = D_MODEL // NUM_HEADS
        EPS = 1e-06

        def _feature_map(x):
            return jax.nn.elu(x) + 1.0
        B, S, D = inputs_q.shape
        H, Dh = (NUM_HEADS, HEAD_DIM)
        q = (inputs_q @ Wq + bq).reshape(B, S, H, Dh)
        k = (inputs_q @ Wk + bk).reshape(B, S, H, Dh)
        v = (inputs_q @ Wv + bv).reshape(B, S, H, Dh)
        q = _feature_map(q)
        k = _feature_map(k)
        kv = jnp.einsum('bkhd,bkhm->bhdm', k, v)
        out = jnp.einsum('bqhd,bhdm->bqhm', q, kv)
        normalizer = jnp.einsum('bqhd,bkhd->bqh', q, k)
        normalizer = jnp.maximum(normalizer, EPS)
        out = out / normalizer[..., None]
        out = out.reshape(B, S, D)
        return out @ Wo + bo

    def _L0_ffn_ref(x, w_in, w_out, w1, w2, wg, we, gb, eb):
        import jax, jax.numpy as jnp
        import numpy as np
        MODEL_DIM = 256
        HIDDEN = 512
        NUM_GROUPS = 2
        EXPERTS_PER_GP = 4
        NUM_EXPERTS = NUM_GROUPS * EXPERTS_PER_GP
        TOP_K = 2
        B, T = (2, 512)

        def _swiglu(x):
            a, b = jnp.split(x, 2, axis=-1)
            return jax.nn.silu(a) * b
        Bs, Ts, C = x.shape
        S = Bs * Ts
        flat = x.reshape(S, C)
        shared = _swiglu(flat @ w_in.T) @ w_out.T
        g_probs = jax.nn.softmax(flat @ wg.T + gb, axis=-1)
        g_idx = jnp.argmax(g_probs, axis=-1)
        e_logits = flat @ we.T + eb
        egid = jnp.arange(NUM_EXPERTS) // EXPERTS_PER_GP
        masked = jnp.where(g_idx[:, None] == egid[None, :], e_logits, -jnp.inf)
        e_probs = jax.nn.softmax(masked, axis=-1)
        g_prob = jnp.take_along_axis(g_probs, g_idx[:, None], axis=1)
        p_expert = e_probs * g_prob
        topv, topi = jax.lax.top_k(p_expert, TOP_K)
        w_se = jnp.zeros((S, NUM_EXPERTS), x.dtype).at[jnp.arange(S)[:, None], topi].add(topv)
        h = _swiglu(flat @ w1.T)
        routed = jnp.zeros_like(shared)
        for e in range(NUM_EXPERTS):
            routed = routed + h * w_se[:, e:e + 1] @ w2[e].T
        return (shared + routed).reshape(Bs, Ts, C)
    x = L0_attn_inputs_q
    xn = _layernorm(x, axis=-1)
    x = x + _L0_attn_ref(xn, L0_attn_Wq, L0_attn_bq, L0_attn_Wk, L0_attn_bk, L0_attn_Wv, L0_attn_bv, L0_attn_Wo, L0_attn_bo) + _L0_ffn_ref(xn, L0_ffn_w_in, L0_ffn_w_out, L0_ffn_w1, L0_ffn_w2, L0_ffn_wg, L0_ffn_we, L0_ffn_gb, L0_ffn_eb)
    return x

_drawn_inputs = setup_inputs


def setup_inputs(seed=0):
    import zlib

    import numpy as np

    out = dict(_drawn_inputs(seed))
    spreads = {'L0_attn_bq': (0.0, 2.0),
     'L0_attn_bk': (0.0, 2.0),
     'L0_attn_bv': (0.0, 0.8),
     'L0_attn_bo': (0.0, 0.8),
     'L0_ffn_gb': (0.0, 0.8),
     'L0_ffn_eb': (0.0, 0.8)}
    factors = {'L0_attn_Wq': 55.32,
     'L0_attn_Wk': 28.52,
     'L0_ffn_w1': 8.0,
     'L0_ffn_w2': 8.0,
     'L0_ffn_wg': 8.0,
     'L0_ffn_we': 8.0,
     'L0_attn_Wv': 8.0,
     'L0_attn_Wo': 5.575,
     'L0_ffn_w_in': 8.0,
     'L0_ffn_w_out': 8.0}
    for name, (base, spread) in spreads.items():
        noise = np.random.default_rng([zlib.crc32(name.encode()), seed]).standard_normal(out[name].shape)
        drawn = base * np.exp(spread * noise) if base else spread * noise
        out[name] = jnp.asarray(drawn.astype(out[name].dtype))
    for name, factor in factors.items():
        out[name] = (out[name] * factor).astype(out[name].dtype)
    return out
```

```python
import numpy as np
import concourse.bass as bass
from concourse import mybir
from contextlib import ExitStack


def layer_program(nc, x, w_kv, w_q, w_o, w_in, w_out, w_exp, w_rt, b_q, b_v, b_k, b_o, b_rt,
                  c_ident, c_tri, c_head, c_heads, c_spread, c_row, c_before, c_part, out):
    f32, f32r, bf16, i32 = mybir.dt.float32, mybir.dt.float32r, mybir.dt.bfloat16, mybir.dt.int32
    ALU = mybir.AluOpType
    ACT = mybir.ActivationFunctionType
    AX = mybir.AxisListType.X

    P = 128
    B, S, D = 16, 512, 256
    N = B * S
    TB = S // P
    DC = D // P
    HC = 4
    E = 8
    NCLS = 12
    NSLOT = 32
    NT = 76
    NG = NT // TB
    SENT = NCLS * N
    ROWS = SENT + P
    UNIT = (2 * 1024 + E * HC * D) // B
    EPS_LN, EPS_N = 1e-5, 1e-6

    xn_d = nc.dram_tensor("xn_d", (N + P, D), f32, kind="Internal").ap()
    base_d = nc.dram_tensor("base_d", (N + P, D), f32, kind="Internal").ap()
    tab_d = nc.dram_tensor("tab_d", (ROWS, 4), i32, kind="Internal").ap()

    ctx = ExitStack()
    with ctx:
        def sb(name, shape, dt):
            return ctx.enter_context(nc.sbuf_tensor(name, shape, dt))

        def sem(name):
            return ctx.enter_context(nc.semaphore(name))

        def pair(name, shape):
            return sb(name + "_hi", shape, f32r), sb(name + "_lo", shape, f32r)

        wkv_hi, wkv_lo = pair("wkv", [P, DC, 512])
        wq_hi, wq_lo = pair("wq", [P, DC, D])
        win_hi, win_lo = pair("win", [P, DC, 1024])
        wout_hi, wout_lo = pair("wout", [P, HC, D])
        wexp_hi, wexp_lo = pair("wexp", [P, B * UNIT])
        wo = sb("wo", [P, DC, D], f32)
        wrt = sb("wrt", [P, DC, 10], f32)
        wstage = sb("wstage", [P, UNIT], f32)

        xt = sb("xt", [P, TB, D], f32)
        res = sb("res", [P, TB, D], f32)
        xn = sb("xn", [P, TB, D], f32)
        xnT_hi, xnT_lo = pair("xnT", [P, DC, S])
        kb = sb("kb", [P, TB, D], f32)
        expt = sb("expt", [P, 2, 512], f32)
        relut = sb("relut", [P, 2, 512], f32)
        phik = sb("phik", [P, TB, D], f32)
        v = sb("v", [P, TB, D], f32)
        qn = v[:, :, :].rearrange("p t n -> p (t n)").rearrange("p (c s) -> p c s", c=DC)
        phiq = sb("phiq", [P, DC, S], f32)
        qn_hi, qn_lo = pair("qn", [P, DC, S])
        gated = sb("gated", [P, 2, S], f32)
        h_hi, h_lo = pair("h", [P, HC, S])
        m_hi, m_lo = pair("m", [P, DC, D])
        r16_hi, r16_lo = qn_hi[0:16, 1, :], qn_lo[0:16, 1, :]

        ident = sb("ident", [P, P], f32)
        triones = sb("triones", [P, 2, P], bf16)
        tri_f = relut[:, 0, 0:P]
        head = sb("head", [P, P], f32)
        heads = sb("heads", [P, DC, 16], f32)
        spread = sb("spread", [16, DC, P], f32r)
        spread_f = relut[0:16, 0, P:3 * P].rearrange("p (c n) -> p c n", c=DC)
        NROW = 16 + 3 * NSLOT
        crow = sb("crow", [P, NROW], f32)
        cpart = sb("cpart", [P, 6], f32)
        bq = sb("bq", [P, DC], f32)
        nbq = sb("nbq", [P, DC], f32)
        bv = sb("bv", [P, DC], f32)
        bk = sb("bk", [P, D], f32)
        bo = sb("bo", [P, D], f32)
        brt = sb("brt", [P, 10], f32)

        stats = sb("stats", [P, TB, 6], f32)
        mv = sb("mv", [P, TB, 2], f32)
        var = sb("var", [P, TB], f32)
        mhalf = sb("mhalf", [P, TB], f32)
        rstd = sb("rstd", [P, TB], f32)
        ksum = sb("ksum", [P, DC], f32)
        khead = sb("khead", [P, DC, 16], f32)
        kvm = relut[:, 0, 0:DC * P].rearrange("p (c n) -> p c n", c=DC)
        kblk = relut[:, 0, DC * P:2 * DC * P].rearrange("p (c n) -> p c n", c=DC)
        kvT = relut[:, 1, 0:DC * P].rearrange("p (c n) -> p c n", c=DC)
        onec = sb("onec", [P, 1], f32)
        rn = sb("rn", [P, TB, 16], f32)

        lg = sb("lg", [P, TB, 10], f32)
        lmax = sb("lmax", [P, TB, 3], f32)
        ex = sb("ex", [P, TB, 10], f32)
        gg = sb("gg", [P, TB, 2], f32)
        gsum = sb("gsum", [P, TB], f32)
        exs = sb("exs", [P, TB, 2, 4], f32)
        w4 = sb("w4", [P, TB, 4], f32)
        esum = sb("esum", [P, TB], f32)
        cmp = sb("cmp", [P, TB, 4, 4], f32)
        cmq = sb("cmq", [P, TB, 4, 4], f32)
        win = sb("win", [P, TB, 4], f32)
        oh = sb("oh", [P, TB, NSLOT], bf16)
        rank = sb("rank", [P, TB + 1, NSLOT], f32)
        run = sb("run", [P, NSLOT], f32)
        pos = sb("pos", [P, TB], f32)
        pos_i = sb("pos_i", [P, TB], i32)
        tok = sb("tok", [P, TB], f32)
        rows = sb("rows", [P, TB, 4], i32)
        fill = relut[:, 1, 0:4 * N // P].bitcast(i32).rearrange("p (n w) -> p n w", w=4)
        cnt = sb("cnt", [P, NSLOT], f32)
        cnt_i = sb("cnt_i", [P, NSLOT], i32)
        first = sb("first", [P, NSLOT], f32)
        memb = sb("memb", [P, NSLOT], f32)
        memt = sb("memt", [P, 3, NSLOT], f32)
        info = sb("info", [P, 4], f32)
        info_i = sb("info_i", [1, 3, NT], i32)
        tab = phik[:, :, :].rearrange("p t d -> p (t d)")[:, 0:4 * NT].bitcast(i32).rearrange("p (n w) -> p n w", w=4)
        idx_next = sb("idx_next", [P, TB], i32)
        cur = sb("cur", [P, TB, 4], i32)
        idx_cur = sb("idx_cur", [P, TB], i32)

        pair_mask = crow[:, 0:16]
        slot_row = crow[:, 16:16 + NSLOT]
        slot_ea = crow[:, 16 + NSLOT:16 + 2 * NSLOT]
        slot_eb = crow[:, 16 + 2 * NSLOT:16 + 3 * NSLOT]
        before = xt[:, :, :].rearrange("p t d -> p (t d)").rearrange("p (a c) -> p a c", a=NSLOT)
        part128 = cpart[:, 0:1]
        part = cpart[:, 1:2]
        tok0 = cpart[:, 2:6]

        bank = [ctx.enter_context(nc.psum_tensor(f"bank{i}", [P, 512], f32)) for i in range(8)]

        setup_ld = sem("setup_ld")
        x_ld = sem("x_ld")
        w_ld = sem("w_ld")
        xn_st = sem("xn_st")
        base_st = sem("base_st")
        fill_st = sem("fill_st")
        w_split = sem("w_split")
        w_round = sem("w_round")
        fill_set = sem("fill_set")
        const_set = sem("const_set")
        passed = sem("passed")
        v_link = sem("v_link")
        g_link = sem("g_link")
        wexp_split = sem("wexp_split")
        t_done = sem("t_done")
        l_done = sem("l_done")
        kv_done = sem("kv_done")
        q_done = sem("q_done")
        hid_done = sem("hid_done")
        acc_done = sem("acc_done")
        rt_done = sem("rt_done")
        nb_done = sem("nb_done")
        m_done = sem("m_done")
        y_done = sem("y_done")
        info_done = sem("info_done")
        thi = sem("thi")
        v_rdy = sem("v_rdy")
        ek_rdy = sem("ek_rdy")
        eq_rdy = sem("eq_rdy")
        ex_rdy = sem("ex_rdy")
        neg_rdy = sem("neg_rdy")
        sil_rdy = sem("sil_rdy")
        hhi_rdy = sem("hhi_rdy")
        rhi_rdy = sem("rhi_rdy")
        qhi_rdy = sem("qhi_rdy")
        mhi_rdy = sem("mhi_rdy")
        xn_rdy = sem("xn_rdy")
        tlo = sem("tlo")
        kb_rdy = sem("kb_rdy")
        phik_rdy = sem("phik_rdy")
        phiq_rdy = sem("phiq_rdy")
        lg_rdy = sem("lg_rdy")
        oh_rdy = sem("oh_rdy")
        gate_rdy = sem("gate_rdy")
        kblk_rdy = sem("kblk_rdy")
        kvT_rdy = sem("kvT_rdy")
        row_rdy = sem("row_rdy")
        rn_rdy = sem("rn_rdy")
        rlo_rdy = sem("rlo_rdy")
        qn_rdy = sem("qn_rdy")
        qlo_rdy = sem("qlo_rdy")
        mlo_rdy = sem("mlo_rdy")
        base_rdy = sem("base_rdy")
        info_rdy = sem("info_rdy")
        kstep = sem("kstep")
        t_link = sem("t_link")
        ystep = sem("ystep")
        infoi_rdy = sem("infoi_rdy")
        rstd_rdy = sem("rstd_rdy")
        res_rdy = sem("res_rdy")
        hlo_rdy = sem("hlo_rdy")
        row_st = sem("row_st")
        tab_ld = sem("tab_ld")
        tab_ld2 = sem("tab_ld2")
        xs_ld = sem("xs_ld")
        bs_ld = sem("bs_ld")
        out_st = sem("out_st")
        idxn_rdy = sem("idxn_rdy")
        idxc_rdy = sem("idxc_rdy")
        cur_rdy = sem("cur_rdy")
        st_done = sem("st_done")
        shid_done = sem("shid_done")
        sw_done = sem("sw_done")
        sthi = sem("sthi")
        stlo = sem("stlo")
        ssil = sem("ssil")
        sgate = sem("sgate")
        shhi = sem("shhi")
        shlo = sem("shlo")
        ysum = sem("ysum")

        block = ctx.enter_context(nc.Block())

        def wait(e, s, n):
            if not isinstance(n, int) or n > 0:
                e.wait_ge(s, n)

        def wait_apart(e, s, n):
            wait(e, s, n)
            if not isinstance(n, int):
                e.sem_inc(passed, 1)

        def rounds(e, body, n):
            body(0, False)
            with e.Fori(1, n - 1) as i:
                body(i, False)
            body(n - 1, True)

        stage = [
            (kb[:, :, :].rearrange("p t n -> p (t n)"), w_kv, wkv_hi, wkv_lo, "p c n -> p (c n)"),
            (v[:, 0:2, :].rearrange("p t n -> p (t n)"), w_q, wq_hi, wq_lo, "p c n -> p (c n)"),
            (phik[:, :, :].rearrange("p t n -> p (t n)"), w_in[:, 0, :], win_hi[:, 0, :], win_lo[:, 0, :], None),
            (phiq[:, :, :].rearrange("p t n -> p (t n)"), w_in[:, 1, :], win_hi[:, 1, :], win_lo[:, 1, :], None),
            (gated[:, :, :].rearrange("p t n -> p (t n)"), w_out, wout_hi, wout_lo, "p c n -> p (c n)"),
        ]

        def x_rows(b):
            return x[bass.ds(b, 1), :, :].rearrange("o (t p) d -> p (o t) d", p=P)

        def rows_of(d, b):
            return d[bass.ds(b * S, S), :].rearrange("(t p) d -> p t d", p=P)

        zero_rows = wexp_lo[:, 0:D].bitcast(f32)

        def mm3(e, to, w_hi, w_lo, m_hi_, m_lo_, first_, last_, free=False):
            e.matmul(to, w_hi, m_hi_, start=first_, stop=False, skip_group_check=free)
            e.matmul(to, w_hi, m_lo_, start=False, stop=False, skip_group_check=free)
            return e.matmul(to, w_lo, m_hi_, start=False, stop=last_, skip_group_check=free)

        @block.sync
        def _(sp):
            sp.dma_start(xt[:, :, :], x[0, :, :].rearrange("(t p) d -> p t d", p=P)).then_inc(x_ld, 16)
            for to, of in ((ident[:], c_ident), (tri_f, c_tri), (head[:], c_head), (heads[:], c_heads), (spread_f, c_spread),
                           (crow[:], c_row), (cpart[:], c_part), (bq[:], b_q), (bv[:], b_v), (bk[:], b_k), (bo[:], b_o), (brt[:], b_rt),
                           (wo[:], w_o), (wrt[:], w_rt)):
                sp.dma_start(to, of).then_inc(setup_ld, 16)
            for buf, of, _, _, flat in stage:
                sp.dma_start(buf, of.rearrange(flat) if flat else of).then_inc(setup_ld, 16)
            sp.wait_ge(fill_set, 3)
            for c in range(NCLS):
                sp.dma_start(tab_d[c * N:(c + 1) * N, :].rearrange("(p n) w -> p n w", p=P), fill[:, :, :]).then_inc(fill_st, 16)
            sp.dma_start(tab_d[SENT:ROWS, :], fill[:, 0, :]).then_inc(fill_st, 16)
            sp.dma_start(xn_d[N:N + P, :], zero_rows).then_inc(fill_st, 16)
            sp.dma_start(base_d[N:N + P, :], zero_rows).then_inc(fill_st, 16)

            def load_store(b, last):
                wait(sp, wexp_split, b)
                sp.dma_start(wstage[:, :], w_exp[:, bass.ds(b * UNIT, UNIT)]).then_inc(w_ld, 16)
                if not last:
                    sp.wait_ge(res_rdy, b + 1)
                    sp.wait_ge(xn_rdy, b + 1)
                    sp.dma_start(xt[:, :, :], x_rows(b + 1)).then_inc(x_ld, 16)
                    sp.wait_ge(xn_rdy, b + 2)
                    sp.dma_start(rows_of(xn_d, b + 1), xn[:, :, :]).then_inc(xn_st, 16)
                else:
                    sp.wait_ge(res_rdy, B)
                    sp.dma_start(before, c_before).then_inc(x_ld, 16)
                sp.wait_ge(base_rdy, DC * (b + 1))
                sp.dma_start(rows_of(base_d, b), res[:, :, :]).then_inc(base_st, 16)

            sp.wait_ge(xn_rdy, 1)
            sp.dma_start(rows_of(xn_d, 0), xn[:, :, :]).then_inc(xn_st, 16)
            rounds(sp, load_store, B)

            sp.wait_ge(infoi_rdy, 1)
            sp.wait_ge(row_st, 16 * TB * B)
            sp.wait_ge(fill_st, 16 * (NCLS + 3))
            for t in range(TB):
                at = sp.value_load(info_i[0:1, 2, t:t + 1], min_val=0, max_val=SENT)
                sp.dma_start(tab[:, t, :], tab_d[bass.ds(at, P), :]).then_inc(tab_ld, 16)
            with sp.Fori(TB, NT) as t:
                at = sp.value_load(info_i[0:1, 2, bass.ds(t, 1)], min_val=0, max_val=SENT)
                sp.dma_start(tab[:, bass.ds(t, 1), :].rearrange("p t w -> p (t w)"), tab_d[bass.ds(at, P), :]).then_inc(tab_ld2, 16)
            sp.wait_ge(xn_st, 16 * B)
            sp.wait_ge(base_st, 16 * B)

        @block.tensor
        def _(pe):
            def transposes(banks, done, free_sem, free_of, ready, ready_n):
                pe.wait_ge(ready, ready_n)
                for c in range(DC):
                    wait(pe, free_sem[c], free_of[c])
                    for t in range(TB):
                        mm = pe.transpose(bank[banks[c]][:, t * P:(t + 1) * P], xn[:, t, c * P:(c + 1) * P], ident[:, :])
                    mm.then_inc(done, 1)

            def logits(b):
                pe.wait_ge(tlo, DC * (b + 1))
                wait(pe, qn_rdy, DC * b)
                for t in range(TB):
                    for c in range(DC):
                        for part_, src in enumerate((xnT_hi, xnT_lo)):
                            mm = pe.matmul(bank[7][:, 10 * t:10 * t + 10], src[:, c, t * P:(t + 1) * P].bitcast(f32),
                                           wrt[:, c, :], start=(c == 0 and part_ == 0), stop=(c == DC - 1 and part_ == 1))
                mm.then_inc(l_done, 1)

            def hidden(j, banks, n, frees, w_hi, w_lo, done):
                for half in range(2):
                    if half == 0:
                        wait(pe, frees[0][0], frees[0][1])
                    else:
                        wait(pe, frees[1][0], frees[1][1])
                    for c in range(DC):
                        lo = half * 512 + j * P
                        mm = mm3(pe, bank[banks[half]][:, :], w_hi[:, c, lo:lo + P], w_lo[:, c, lo:lo + P],
                                 xnT_hi[:, c, :], xnT_lo[:, c, :], c == 0, c == DC - 1)
                mm.then_inc(done, 1)

            def batch(b, last):
                for t in range(TB):
                    if t == 0:
                        pe.wait_ge(tlo, DC * (b + 1))
                        wait(pe, sil_rdy, HC * b)
                    elif t == 1:
                        wait(pe, gate_rdy, HC * b)
                    for c in range(DC):
                        mm = mm3(pe, bank[t][:, :], xnT_hi[:, c, t * P:(t + 1) * P], xnT_lo[:, c, t * P:(t + 1) * P],
                                 wkv_hi[:, c, :], wkv_lo[:, c, :], c == 0, c == DC - 1)
                    mm.then_inc(kv_done, 1)
                for o in range(DC):
                    if o == 0:
                        wait(pe, mlo_rdy, b)
                    else:
                        wait(pe, base_rdy, DC * b - 1)
                    for c in range(DC):
                        mm = mm3(pe, bank[4 + o][:, :], wq_hi[:, c, o * P:(o + 1) * P], wq_lo[:, c, o * P:(o + 1) * P],
                                 xnT_hi[:, c, :], xnT_lo[:, c, :], c == 0, c == DC - 1)
                    mm.then_inc(q_done, 1)
                hidden(0, (6, 7), b, ((base_rdy, DC * b), (lg_rdy, 2 * b + 1)), win_hi, win_lo, hid_done)
                pe.wait_ge(v_rdy, TB * b + 2)         
                hidden(1, (0, 1), b, ((kb_rdy, TB * b + 1), (kb_rdy, TB * b + 2)), win_hi, win_lo, hid_done)
                pe.wait_ge(phik_rdy, 2 * (b + 1))
                pe.wait_ge(v_rdy, TB * (b + 1))
                for c in range(DC):
                    for t in range(TB):
                        pe.matmul(bank[2][:, c * P:(c + 1) * P], v[:, t, c * P:(c + 1) * P], phik[:, t, c * P:(c + 1) * P],
                                  start=(t == 0), stop=(t == TB - 1))
                for c in range(DC):
                    for t in range(TB):
                        mm = pe.matmul(bank[2][:, 256 + c:257 + c], phik[:, t, c * P:(c + 1) * P], onec[:, :],
                                       start=(t == 0), stop=(t == TB - 1))
                mm.then_inc(acc_done, 1)
                hidden(2, (3, 4), b, ((kb_rdy, TB * (b + 1)), (eq_rdy, DC * b + 1)), win_hi, win_lo, hid_done)
                pe.wait_ge(kblk_rdy, b + 1)
                pe.wait_ge(eq_rdy, DC * (b + 1))
                for c in range(DC):
                    pe.matmul(bank[5][:, c * P:(c + 1) * P], kblk[:, c, :], ident[:, :], start=True, stop=True)
                pe.wait_ge(oh_rdy, b + 1)
                W = NSLOT
                pe.matmul(bank[5][:, 256:256 + TB * W], triones[:, 0, :], oh[:, :, :].rearrange("p t c -> p (t c)"),
                          start=True, stop=False, skip_group_check=True)
                for n in range(TB, 0, -1):
                    o = 256 + (TB + 1 - n) * W
                    mm = pe.matmul(bank[5][:, o:o + n * W], triones[:, 1, :], oh[:, 0:n, :].rearrange("p t c -> p (t c)"),
                                   start=False, stop=(n == 1), skip_group_check=True)
                mm.then_inc(rt_done, 1)
                pe.wait_ge(phiq_rdy, DC * (b + 1))
                pe.wait_ge(gate_rdy, HC * b + 1)
                for t in range(TB):
                    for c in range(DC):
                        mm = pe.matmul(bank[6][:, 16 * t:16 * t + 16], phiq[:, c, t * P:(t + 1) * P], khead[:, c, :],
                                       start=(c == 0), stop=(c == DC - 1))
                mm.then_inc(nb_done, 1)
                hidden(3, (0, 1), b, ((sil_rdy, HC * b + 2), (gate_rdy, HC * b + 2)), win_hi, win_lo, hid_done)
                pe.wait_ge(rn_rdy, b + 1)
                for t in range(TB):
                    mm = pe.transpose(bank[7][0:16, t * P:(t + 1) * P], rn[:, t, :], ident[:, :])
                mm.then_inc(nb_done, 1)
                pe.wait_ge(kvT_rdy, b + 1)
                pe.wait_ge(gate_rdy, HC * b + 3)
                for c in range(DC):
                    mm = pe.matmul(bank[4][:, c * D:(c + 1) * D], kvT[:, c, :], wo[:, c, :], start=True, stop=True)
                mm.then_inc(m_done, 1)
                if not last:
                    transposes((2, 3), t_done, (kblk_rdy, sil_rdy), (b + 1, HC * b + 3), xn_rdy, b + 2)
                else:
                    pe.wait_ge(info_rdy, 1)
                    for n in range(3):
                        mm = pe.matmul(bank[2][0:1, n * NT:(n + 1) * NT], info[0:NT, n:n + 1], ident[0:NT, 0:NT],
                                       start=True, stop=True)
                    mm.then_inc(info_done, 1)
                pe.wait_ge(rlo_rdy, b + 1)
                for c in range(DC):
                    pe.matmul(bank[6 + c][:, :], spread[:, c, :], r16_hi, start=True, stop=False)
                    mm = pe.matmul(bank[6 + c][:, :], spread[:, c, :], r16_lo, start=False, stop=True)
                    mm.then_inc(nb_done, 1)
                def y(t):
                    return bank[5 + t // 2][:, (t % 2) * D:(t % 2 + 1) * D]
                pe.wait_ge(row_rdy, b + 1)
                pe.wait_ge(kvT_rdy, b + 1)
                pe.wait_ge(hlo_rdy, HC * b + 3)
                for t in range(TB):
                    if t == 2:
                        pe.wait_ge(qn_rdy, DC * b + 1)
                    for j in range(HC - 1):
                        mm3(pe, y(t), h_hi[:, j, t * P:(t + 1) * P], h_lo[:, j, t * P:(t + 1) * P],
                            wout_hi[:, j, :], wout_lo[:, j, :], t % 2 == 0 and j == 0, False, True)
                pe.wait_ge(mlo_rdy, b + 1)
                pe.wait_ge(qlo_rdy, DC * (b + 1))
                for t in range(TB):
                    for c in range(DC):
                        mm3(pe, y(t), qn_hi[:, c, t * P:(t + 1) * P], qn_lo[:, c, t * P:(t + 1) * P],
                            m_hi[:, c, :], m_lo[:, c, :], False, False, True)
                pe.wait_ge(hlo_rdy, HC * (b + 1))
                for t in range(TB):
                    mm = mm3(pe, y(t), h_hi[:, 3, t * P:(t + 1) * P], h_lo[:, 3, t * P:(t + 1) * P],
                             wout_hi[:, 3, :], wout_lo[:, 3, :], False, True, True)
                    if t % 2 == 1:
                        mm.then_inc(y_done, 1)
                if not last:
                    logits(b + 1)

            pe.wait_ge(const_set, 3)
            pe.wait_ge(setup_ld, 16 * (14 + len(stage)))
            transposes((2, 3), t_done, (t_done, t_done), (0, 0), xn_rdy, 1)
            logits(0)
            pe.wait_ge(w_split, 1)
            rounds(pe, batch, B)

            w1_hi = wexp_hi[:, 0:2048].rearrange("p (c n) -> p c n", c=DC)
            w1_lo = wexp_lo[:, 0:2048].rearrange("p (c n) -> p c n", c=DC)
            pe.wait_ge(wexp_split, B)
            pe.wait_ge(infoi_rdy, 1)
            pe.wait_ge(tlo, DC * B)
            transposes((1, 2), st_done, (gate_rdy, infoi_rdy), (HC * B, 1), xs_ld, 16 * TB)

            def group(g, last):
                pe.wait_ge(stlo, DC * (g + 1))
                hidden(0, (0, 1), g, ((sgate, HC * g), (stlo, DC * g + 1)), w1_hi, w1_lo, shid_done)
                hidden(1, (2, 3), g, ((stlo, DC * (g + 1)), (ysum, TB * g - 3)), w1_hi, w1_lo, shid_done)
                wait(pe, ysum, TB * g - 1)
                if isinstance(g, int) and g == 0:
                    pe.wait_ge(base_rdy, DC * B)
                hidden(2, (4, 5), g, ((ysum, TB * g - 2), (ysum, TB * g - 1)), w1_hi, w1_lo, shid_done)
                hidden(3, (6, 0), g, ((ysum, TB * g), (ssil, HC * g + 1)), w1_hi, w1_lo, shid_done)
                if not last:
                    transposes((1, 2), st_done, (sgate, ssil), (HC * g + 1, HC * g + 2), xs_ld, 16 * TB * (g + 2))
                at = [[pe.value_load(info_i[0:1, n, bass.ds(g * TB + t, 1)], min_val=0, max_val=(E - 1) * HC * D)
                       for n in range(2)] for t in range(TB)]
                free = ((sgate, HC * g + 2), (ssil, HC * g + 3), (sgate, HC * g + 3), (ssil, HC * g + 4))

                def second(t, js, start, stop):
                    for n in range(2):
                        for j in js:
                            off = at[t][n] + (2048 + j * D)
                            r_hi = wexp_hi[:, bass.ds(off, D)]
                            r_lo = wexp_lo[:, bass.ds(off, D)]
                            mm = mm3(pe, bank[3 + t][:, n * D:(n + 1) * D], h_hi[:, j, t * P:(t + 1) * P],
                                     h_lo[:, j, t * P:(t + 1) * P], r_hi, r_lo, start and n == 0 and j == 0, stop, True)
                    return mm
                pe.wait_ge(shlo, HC * g + 3)
                for t in range(TB):
                    pe.wait_ge(*free[t])
                    second(t, range(HC - 1), True, False)
                pe.wait_ge(shlo, HC * (g + 1))
                for t in range(TB):
                    second(t, (HC - 1,), False, True).then_inc(sw_done, 1)

            rounds(pe, group, NG)

        @block.scalar
        def _(act):
            act.wait_ge(setup_ld, 16 * (14 + len(stage)))
            for buf, _, hi, _, flat in stage:
                act.copy(hi[:].rearrange(flat) if flat else hi, buf).then_inc(w_round, 1)

            def t_high(b):
                for c in range(DC):
                    act.wait_ge(t_done, DC * b + c + 1)
                    wait(act, hid_done, HC * b)
                    wait(act, l_done, b)
                    act.copy(xnT_hi[:, c, :], bank[2 + c][:, :]).then_inc(thi, 1)

            def silu(j, n, hid, gate_bank, lo_prev, sil, first_wait=None):
                act.wait_ge(hid, n + 1)
                wait(act, lo_prev, n - 1)
                act.activation(gated[:, j % 2, :], bank[gate_bank][:, :], ACT.Silu).then_inc(sil, 1)

            def high(j, n, gate, hhi):
                act.wait_ge(gate, n + 1)
                act.copy(h_hi[:, j, :], gated[:, j % 2, :]).then_inc(hhi, 1)

            def batch(b, last):
                for t in range(TB):
                    act.wait_ge(kb_rdy, TB * b + t + 1)
                    wait(act, qlo_rdy, DC * b)
                    act.copy(v[:, t, :], bank[t][:, D:2 * D]).then_inc(v_rdy, 1)
                for i in range(2):
                    act.wait_ge(kb_rdy, TB * b + 2 * i + 2)
                    wait(act, phiq_rdy, DC * (b - 1) + i + 1)
                    src = kb[:, 2 * i:2 * i + 2, :].rearrange("p t n -> p (t n)")
                    act.activation(expt[:, i, :], src, ACT.Relu, scale=-1.0).then_inc(neg_rdy, 1)
                    act.wait_ge(neg_rdy, 4 * b + i + 1)
                    act.activation(expt[:, i, :], expt[:, i, :], ACT.Exp, scale=-1.0).then_inc(ek_rdy, 1)
                for o in range(DC):
                    act.wait_ge(q_done, DC * b + o + 1)
                    act.wait_ge(phik_rdy, 2 * b + o + 1)
                    act.activation(expt[:, o, :], bank[4 + o][:, :], ACT.Relu, bias=nbq[:, o:o + 1], scale=-1.0).then_inc(neg_rdy, 1)
                    act.activation(relut[:, o, :], bank[4 + o][:, :], ACT.Relu, bias=bq[:, o:o + 1])
                    act.wait_ge(neg_rdy, 4 * b + o + 3)
                    act.activation(expt[:, o, :], expt[:, o, :], ACT.Exp, scale=-1.0).then_inc(eq_rdy, 1)
                act.wait_ge(lg_rdy, 2 * b + 2)
                act.activation(ex[:, :, :], lg[:, :, :], ACT.Exp).then_inc(ex_rdy, 1)
                wait(act, y_done, DC * b)
                gates = (6, 0, 3, 0)
                for j in (0, 1, 2):
                    silu(j, HC * b + j, hid_done, gates[j], hlo_rdy, sil_rdy)
                    high(j, HC * b + j, gate_rdy, hhi_rdy)
                act.wait_ge(nb_done, 4 * b + 2)
                act.copy(r16_hi, bank[7][0:16, :]).then_inc(rhi_rdy, 1)
                silu(3, HC * b + 3, hid_done, gates[3], hlo_rdy, sil_rdy)
                high(3, HC * b + 3, gate_rdy, hhi_rdy)
                act.wait_ge(m_done, b + 1)
                act.copy(m_hi[:, :, :].rearrange("p c n -> p (c n)"), bank[4][:, :]).then_inc(mhi_rdy, 1)
                for c in range(DC):
                    act.wait_ge(qn_rdy, DC * b + c + 1)
                    act.copy(qn_hi[:, c, :], qn[:, c, :]).then_inc(qhi_rdy, 1)
                if not last:
                    t_high(b + 1)

            t_high(0)
            act.wait_ge(fill_st, 16 * (NCLS + 3))
            rounds(act, batch, B)

            def st_high(g):
                for c in range(DC):
                    act.wait_ge(st_done, DC * g + c + 1)
                    wait(act, shid_done, HC * g)
                    act.copy(xnT_hi[:, c, :], bank[1 + c][:, :]).then_inc(sthi, 1)

            def group(g, last):
                gates = (0, 2, 4, 6)
                wait(act, sw_done, TB * g)
                for j in range(HC):
                    silu(j, HC * g + j, shid_done, gates[j], shlo, ssil)
                    high(j, HC * g + j, sgate, shhi)
                if not last:
                    st_high(g + 1)

            act.wait_ge(hid_done, HC * B)
            act.wait_ge(y_done, DC * B)
            act.wait_ge(hlo_rdy, HC * B)
            st_high(0)
            rounds(act, group, NG)

        @block.vector
        def _(dve):
            LN_LINKS, RT_LINKS, RK_LINKS = 3, 26, 4
            PER = LN_LINKS + RT_LINKS + RK_LINKS
            state = [0, 0]

            def start(n):
                state[:] = n, 0

            def link(ins):
                ins.then_inc(v_link, 1)
                state[1] += 1
                dve.wait_ge(v_link, state[0] + state[1])

            def norm(b, base):
                start(base)
                dve.wait_ge(x_ld, 16 * (b + 1))
                for t in range(TB):
                    ins = dve.bn_stats(stats[:, t, :], xt[:, t, :])
                link(ins)
                if not isinstance(b, int):
                    dve.sem_inc(passed, 1)
                for t in range(TB):
                    ins = dve.bn_aggr(mv[:, t, :], stats[:, t, :])
                link(ins)
                link(dve.tensor_scalar(var[:, :], mv[:, :, 1], EPS_LN, None, ALU.add))

            def normalise(b):
                dve.wait_ge(rstd_rdy, b + 1)
                wait(dve, xn_st, 16 * b)
                wait(dve, t_done, DC * b)
                for t in range(TB):
                    ins = dve.tensor_scalar(xn[:, t, :], xt[:, t, :], mv[:, t, 0:1], rstd[:, t:t + 1], ALU.subtract, ALU.mult)
                ins.then_inc(xn_rdy, 1)

            def t_low(b):
                for c in range(DC):
                    dve.wait_ge(thi, DC * b + c + 1)
                    dve.tensor_tensor(xnT_lo[:, c, :], bank[2 + c][:, :], xnT_hi[:, c, :].bitcast(f32), ALU.subtract).then_inc(tlo, 1)

            def logits_in(b):
                dve.wait_ge(l_done, b + 1)
                link(dve.tensor_tensor(lg[:, :, :], bank[7][:, 0:40].rearrange("p (t n) -> p t n", t=TB),
                                       brt[:, :].unsqueeze(1).broadcast_to([P, TB, 10]), ALU.add))
                link(dve.tensor_tensor(lmax[:, :, 0], lg[:, :, 0], lg[:, :, 1], ALU.max))
                link(dve.tensor_reduce(lmax[:, :, 1:3], lg[:, :, 2:10].rearrange("p t (g e) -> p t g e", g=2), AX, ALU.max))
                dve.tensor_tensor(lg[:, :, 0:2], lg[:, :, 0:2], lmax[:, :, 0:1].broadcast_to([P, TB, 2]), ALU.subtract).then_inc(lg_rdy, 1)
                l8 = lg[:, :, 2:10].rearrange("p t (g e) -> p t g e", g=2)
                dve.tensor_tensor(l8, l8, lmax[:, :, 1:3].unsqueeze(3).broadcast_to([P, TB, 2, 4]), ALU.subtract).then_inc(lg_rdy, 1)

            def route(b):
                dve.wait_ge(ex_rdy, b + 1)
                link(dve.tensor_tensor(gg[:, :, 1], ex[:, :, 1], ex[:, :, 0], ALU.is_gt))
                link(dve.tensor_scalar(gg[:, :, 0], gg[:, :, 1], -1.0, 1.0, ALU.mult, ALU.add))
                link(dve.tensor_tensor(gsum[:, :], ex[:, :, 0], ex[:, :, 1], ALU.add))
                g4 = gg[:, :, :].unsqueeze(3).broadcast_to([P, TB, 2, 4])
                link(dve.tensor_tensor(exs[:, :, :, :], ex[:, :, 2:10].rearrange("p t (g e) -> p t g e", g=2), g4, ALU.mult))
                link(dve.tensor_tensor(w4[:, :, :], exs[:, :, 0, :], exs[:, :, 1, :], ALU.add))
                link(dve.tensor_reduce(esum[:, :], w4[:, :, :], AX, ALU.add))
                link(dve.tensor_tensor(esum[:, :], esum[:, :], gsum[:, :], ALU.mult))
                link(dve.reciprocal(gsum[:, :], esum[:, :]))
                link(dve.tensor_tensor(w4[:, :, :], w4[:, :, :], gsum[:, :].unsqueeze(2).broadcast_to([P, TB, 4]), ALU.mult))
                wj = w4[:, :, :].unsqueeze(3).broadcast_to([P, TB, 4, 4])
                wi = w4[:, :, :].unsqueeze(2).broadcast_to([P, TB, 4, 4])
                msk = pair_mask.rearrange("p (j i) -> p j i", j=4).unsqueeze(1).broadcast_to([P, TB, 4, 4])
                link(dve.tensor_tensor(cmp[:, :, :, :], wj, wi, ALU.is_gt))
                link(dve.tensor_tensor(cmq[:, :, :, :], wj, wi, ALU.is_equal))
                link(dve.tensor_tensor(cmq[:, :, :, :], cmq[:, :, :, :], msk, ALU.mult))
                link(dve.tensor_tensor(cmp[:, :, :, :], cmp[:, :, :, :], cmq[:, :, :, :], ALU.add))
                link(dve.tensor_reduce(win[:, :, :], cmp[:, :, :, :], AX, ALU.add))
                link(dve.tensor_scalar(win[:, :, :], win[:, :, :], 2.0, None, ALU.is_ge))
                link(dve.tensor_tensor(cmp[:, :, :, :], win[:, :, :].unsqueeze(3).broadcast_to([P, TB, 4, 4]),
                                       win[:, :, :].unsqueeze(2).broadcast_to([P, TB, 4, 4]), ALU.mult))
                link(dve.tensor_tensor(cmp[:, :, :, :], cmp[:, :, :, :], msk, ALU.mult))
                pr = cmp[:, :, :, :].rearrange("p t j i -> p t (j i)")
                wait(dve, rt_done, b)
                for g in range(2):
                    ins = dve.tensor_tensor(oh[:, :, 16 * g:16 * g + 16], pr, gg[:, :, g:g + 1].broadcast_to([P, TB, 16]), ALU.mult)
                ins.then_inc(oh_rdy, 1)
                wait(dve, row_st, 16 * TB * b)
                wts = rows[:, :, :].bitcast(f32)
                q = cmq[:, :, :, :].rearrange("p t j i -> p t (j i)")
                link(dve.tensor_tensor(cmq[:, :, :, :], cmp[:, :, :, :], wj, ALU.mult))
                link(dve.tensor_reduce(wts[:, :, 1], q, AX, ALU.add))
                link(dve.tensor_tensor(cmq[:, :, :, :], cmp[:, :, :, :], wi, ALU.mult))
                link(dve.tensor_reduce(wts[:, :, 2], q, AX, ALU.add))
                link(dve.tensor_copy(rows[:, :, 0], tok[:, :]))
                link(dve.tensor_scalar(tok[:, :], tok[:, :], float(S), None, ALU.add))

            rank_bank = bank[5][:, 256:256 + 5 * NSLOT].rearrange("p (t c) -> p t c", c=NSLOT)

            def ranks(b):
                dve.wait_ge(rt_done, b + 1)
                link(dve.tensor_tensor(rank[:, :, :], rank_bank, run[:, :].unsqueeze(1).broadcast_to([P, TB + 1, NSLOT]), ALU.add))
                link(dve.tensor_copy(run[:, :], rank[:, TB, :]))
                link(dve.tensor_tensor(rank[:, 0:TB, :], rank[:, 0:TB, :], oh[:, :, :], ALU.mult))
                link(dve.tensor_reduce(pos[:, :], rank[:, 0:TB, :], AX, ALU.add))
                dve.tensor_copy(pos_i[:, :], pos[:, :]).then_inc(row_rdy, 1)

            def gate(j, n, hid, up_bank, sil, out_sem):
                dve.wait_ge(sil, n + 1)
                dve.tensor_tensor(gated[:, j % 2, :], gated[:, j % 2, :], bank[up_bank][:, :], ALU.mult).then_inc(out_sem, 1)

            def batch(b, last):
                base = LN_LINKS + PER * b
                start(base)
                logits_in(b)
                for t in range(TB):
                    dve.wait_ge(kv_done, TB * b + t + 1)
                    wait(dve, ek_rdy, 2 * b)
                    dve.tensor_tensor(kb[:, t, :], bank[t][:, 0:D], bk[:, :], ALU.add).then_inc(kb_rdy, 1)
                for i in range(2):
                    dve.wait_ge(ek_rdy, 2 * b + i + 1)
                    wait(dve, acc_done, b)
                    dve.scalar_tensor_tensor(phik[:, 2 * i:2 * i + 2, :].rearrange("p t n -> p (t n)"),
                                             kb[:, 2 * i:2 * i + 2, :].rearrange("p t n -> p (t n)"), 0.0,
                                             expt[:, i, :], ALU.max, ALU.add).then_inc(phik_rdy, 1)
                for o in range(DC):
                    dve.wait_ge(eq_rdy, DC * b + o + 1)
                    wait(dve, nb_done, 4 * (b - 1) + 1)
                    dve.tensor_tensor(phiq[:, o, :], expt[:, o, :], relut[:, o, :], ALU.add).then_inc(phiq_rdy, 1)
                route(b)
                gate(0, HC * b, hid_done, 7, sil_rdy, gate_rdy)
                gate(1, HC * b + 1, hid_done, 1, sil_rdy, gate_rdy)
                dve.wait_ge(acc_done, b + 1)
                dve.tensor_copy(ksum[:, :], bank[2][:, 256:258]).then_inc(kstep, 1)
                dve.wait_ge(kstep, 2 * b + 1)
                for c in range(DC):
                    dve.tensor_scalar(kblk[:, c, :], head[:, :], ksum[:, c:c + 1], None, ALU.mult)
                    dve.tensor_scalar(khead[:, c, :], heads[:, c, :], ksum[:, c:c + 1], None, ALU.mult)
                dve.tensor_tensor(kvm[:, :, :], bank[2][:, 0:256].rearrange("p (c n) -> p c n", c=DC),
                                  head[:, :].unsqueeze(1).broadcast_to([P, DC, P]), ALU.mult).then_inc(kblk_rdy, 1)
                gate(2, HC * b + 2, hid_done, 4, sil_rdy, gate_rdy)
                dve.wait_ge(rt_done, b + 1)
                dve.wait_ge(kblk_rdy, b + 1)
                wait(dve, m_done, b)
                for c in range(DC):
                    ins = dve.scalar_tensor_tensor(kvT[:, c, :], bank[5][:, c * P:(c + 1) * P], bv[:, c:c + 1], kvm[:, c, :],
                                                   ALU.mult, ALU.add)
                ins.then_inc(kvT_rdy, 1)
                dve.wait_ge(nb_done, 4 * b + 1)
                dve.tensor_scalar(rn[:, :, :].rearrange("p t h -> p (t h)"), bank[6][:, 0:64], EPS_N, None, ALU.max).then_inc(kstep, 1)
                dve.wait_ge(kstep, 2 * b + 2)
                dve.reciprocal(rn[:, :, :], rn[:, :, :]).then_inc(rn_rdy, 1)
                start(base + RT_LINKS)
                ranks(b)
                if not last:
                    start(base + RT_LINKS + RK_LINKS)
                    norm(b + 1, base + RT_LINKS + RK_LINKS)
                dve.wait_ge(rhi_rdy, b + 1)
                dve.tensor_tensor(r16_lo, bank[7][0:16, :], r16_hi.bitcast(f32), ALU.subtract).then_inc(rlo_rdy, 1)
                if not last:
                    normalise(b + 1)
                else:
                    tile_list()
                gate(3, HC * b + 3, hid_done, 1, sil_rdy, gate_rdy)
                dve.wait_ge(mhi_rdy, b + 1)
                mflat = "p c n -> p (c n)"
                dve.tensor_tensor(m_lo[:, :, :].rearrange(mflat), bank[4][:, :], m_hi[:, :, :].rearrange(mflat).bitcast(f32),
                                  ALU.subtract).then_inc(mlo_rdy, 1)
                for c in range(DC):
                    dve.wait_ge(nb_done, 4 * b + 3 + c)
                    dve.tensor_tensor(qn[:, c, :], phiq[:, c, :], bank[6 + c][:, :], ALU.mult).then_inc(qn_rdy, 1)
                for c in range(DC):
                    dve.wait_ge(qhi_rdy, DC * b + c + 1)
                    dve.tensor_tensor(qn_lo[:, c, :], qn[:, c, :], qn_hi[:, c, :].bitcast(f32), ALU.subtract).then_inc(qlo_rdy, 1)
                if not last:
                    t_low(b + 1)
                else:
                    dve.wait_ge(info_done, 1)
                    dve.tensor_copy(info_i[:, :, :].rearrange("p n t -> p (n t)"), bank[2][0:1, 0:3 * NT]).then_inc(infoi_rdy, 1)
                dve.wait_ge(res_rdy, b + 1)
                for n in range(2):
                    dve.wait_ge(y_done, DC * b + n + 1)
                    part_ = res[:, 2 * n:2 * n + 2, :].rearrange("p t d -> p (t d)")
                    dve.tensor_tensor(part_, part_, bank[5 + n][:, :], ALU.add).then_inc(base_rdy, 1)

            def tile_list():
                dve.wait_ge(x_ld, 16 * (B + 1))
                dve.wait_ge(v_link, LN_LINKS + PER * (B - 1) + RT_LINKS + RK_LINKS)

                def step(ins, k):
                    ins.then_inc(t_link, 1)
                    dve.wait_ge(t_link, k)
                step(dve.tensor_tensor(cnt[:, :], run[:, :], slot_row, ALU.subtract), 1)
                step(dve.tensor_scalar(cnt[:, :], cnt[:, :], float(P - 1), None, ALU.add), 2)
                step(dve.tensor_copy(cnt_i[:, :], cnt[:, :]), 3)
                step(dve.tensor_single_scalar(cnt_i[:, :], cnt_i[:, :], 7, ALU.arith_shift_right), 4)
                step(dve.tensor_copy(cnt[:, :], cnt_i[:, :]), 5)
                big = kb[:, :, :].rearrange("p t n -> p (t n)").rearrange("p (a c) -> p a c", a=NSLOT)
                step(dve.tensor_tensor(big, before,
                                       cnt[:, :].unsqueeze(1).broadcast_to([P, NSLOT, NSLOT]), ALU.mult), 6)
                step(dve.tensor_reduce(first[:, :], big, AX, ALU.add), 7)
                step(dve.tensor_tensor(cnt[:, :], cnt[:, :], first[:, :], ALU.add), 8)
                step(dve.tensor_scalar(memb[:, :], first[:, :], part, None, ALU.is_le), 9)
                step(dve.tensor_scalar(cnt[:, :], cnt[:, :], part, None, ALU.is_gt), 10)
                step(dve.tensor_tensor(memb[:, :], memb[:, :], cnt[:, :], ALU.mult), 11)
                step(dve.tensor_tensor(memt[:, 0, :], memb[:, :], slot_ea, ALU.mult), 12)
                step(dve.tensor_tensor(memt[:, 1, :], memb[:, :], slot_eb, ALU.mult), 13)
                step(dve.tensor_scalar(first[:, :], first[:, :], -float(P), part128, ALU.mult, ALU.add), 14)
                step(dve.tensor_tensor(first[:, :], first[:, :], slot_row, ALU.add), 15)
                step(dve.tensor_scalar(first[:, :], first[:, :], -float(SENT), None, ALU.add), 16)
                step(dve.tensor_tensor(memt[:, 2, :], memb[:, :], first[:, :], ALU.mult), 17)
                step(dve.tensor_reduce(info[:, 0:3], memt[:, :, :], AX, ALU.add), 18)
                dve.tensor_scalar(info[:, 2:3], info[:, 2:3], float(SENT), None, ALU.add).then_inc(info_rdy, 1)

            dve.wait_ge(setup_ld, 16 * (14 + len(stage)))
            dve.memset(onec[:, :], 1.0)
            dve.tensor_scalar(nbq[:, :], bq[:, :], -1.0, None, ALU.mult)
            dve.memset(triones[:, 1, :], 1.0)
            dve.tensor_copy(triones[:, 0, :], tri_f)
            dve.tensor_copy(spread[:, :, :], spread_f)
            dve.tensor_copy(run[:, :], slot_row)
            dve.tensor_copy(tok[:, :], tok0).then_inc(const_set, 1)
            dve.wait_ge(const_set, 3)
            norm(0, 0)
            normalise(0)
            for n, (buf, _, hi, lo, flat) in enumerate(stage):
                dve.wait_ge(w_round, n + 1)
                h = (hi[:].rearrange(flat) if flat else hi).bitcast(f32)
                ins = dve.tensor_tensor(lo[:].rearrange(flat) if flat else lo, buf, h, ALU.subtract)
                if n == 1:
                    dve.wait_ge(thi, DC)
                    t_low(0)
            ins.then_inc(w_split, 1)
            rounds(dve, batch, B)

            def st_low(g):
                for c in range(DC):
                    dve.wait_ge(sthi, DC * g + c + 1)
                    dve.tensor_tensor(xnT_lo[:, c, :], bank[1 + c][:, :], xnT_hi[:, c, :].bitcast(f32), ALU.subtract).then_inc(stlo, 1)

            def group(g, last):
                ups = (1, 3, 5, 0)
                for j in range(HC):
                    gate(j, HC * g + j, shid_done, ups[j], ssil, sgate)
                    dve.wait_ge(shhi, HC * g + j + 1)
                    dve.tensor_tensor(h_lo[:, j, :], gated[:, j % 2, :], h_hi[:, j, :].bitcast(f32), ALU.subtract).then_inc(shlo, 1)
                if not last:
                    st_low(g + 1)
                dve.wait_ge(bs_ld, 16 * TB * (g + 1))
                dve.wait_ge(cur_rdy, g + 1)
                wts = cur[:, :, :].bitcast(f32)
                for t in range(TB):
                    dve.wait_ge(sw_done, TB * g + t + 1)
                    dve.scalar_tensor_tensor(res[:, t, :], bank[3 + t][:, 0:D], wts[:, t, 1:2], res[:, t, :],
                                             ALU.mult, ALU.add).then_inc(ystep, 1)
                for t in range(TB):
                    dve.wait_ge(ystep, TB * g + t + 1)
                    dve.scalar_tensor_tensor(res[:, t, :], bank[3 + t][:, D:2 * D], wts[:, t, 2:3], res[:, t, :],
                                             ALU.mult, ALU.add).then_inc(ysum, 1)

            st_low(0)
            rounds(dve, group, NG)

        @block.gpsimd
        def _(pool):
            pool.memset(fill[:, :, 1:4], 0).then_inc(fill_set, 1)
            pool.memset(fill[:, :, 0:1], N).then_inc(fill_set, 1)
            pool.memset(wexp_lo[:, 0:D].bitcast(f32), 0.0).then_inc(fill_set, 1)
            pool.memset(mhalf[:, :], -0.5).then_inc(const_set, 1)
            pool.memset(rows[:, :, 3:4], 0).then_inc(const_set, 1)
            pool.wait_ge(const_set, 3)

            def reciprocal_root(b, count):
                pool.wait_ge(v_link, count)
                pool.tensor_tensor(rstd[:, :], var[:, :], mhalf[:, :], ALU.pow).then_inc(rstd_rdy, 1)

            def low(j, n, hhi, hlo):
                pool.wait_ge(hhi, n + 1)
                pool.tensor_tensor(h_lo[:, j, :], gated[:, j % 2, :], h_hi[:, j, :].bitcast(f32), ALU.subtract).then_inc(hlo, 1)

            def batch(b, last):
                wait(pool, base_st, 16 * b)
                pool.wait_ge(x_ld, 16 * (b + 1))
                pool.wait_ge(setup_ld, 16 * (14 + len(stage)))
                pool.tensor_tensor(res[:, :, :], xt[:, :, :], bo[:, :].unsqueeze(1).broadcast_to([P, TB, D]), ALU.add).then_inc(res_rdy, 1)
                low(0, HC * b, hhi_rdy, hlo_rdy)
                low(1, HC * b + 1, hhi_rdy, hlo_rdy)
                low(2, HC * b + 2, hhi_rdy, hlo_rdy)
                if not last:
                    reciprocal_root(b + 1, 3 + 33 * (b + 1))
                low(3, HC * b + 3, hhi_rdy, hlo_rdy)
                wait_apart(pool, row_rdy, b + 1)
                for t in range(TB):
                    pool.indirect_dma_start(tab_d, bass.IndirectOffsetOnAxis(ap=pos_i[:, t:t + 1], axis=0),
                                            rows[:, t, :], None).then_inc(row_st, 16)
                wait_apart(pool, w_ld, 16 * (b + 1))
                pool.tensor_copy(wexp_hi[:, bass.ds(b * UNIT, UNIT)], wstage[:, :]).then_inc(g_link, 1)
                pool.wait_ge(g_link, b + 1)
                pool.tensor_tensor(wexp_lo[:, bass.ds(b * UNIT, UNIT)], wstage[:, :],
                                   wexp_hi[:, bass.ds(b * UNIT, UNIT)].bitcast(f32), ALU.subtract).then_inc(wexp_split, 1)

            reciprocal_root(0, 3)
            pool.wait_ge(fill_st, 16 * (NCLS + 3))
            rounds(pool, batch, B)

            def gather(d, to, idx, done):
                for t in range(TB):
                    pool.indirect_dma_start(to[:, t, :], None, d, bass.IndirectOffsetOnAxis(ap=idx[:, t:t + 1], axis=0)).then_inc(done, 16)

            def tokens(g):
                wait_apart(pool, xs_ld, 16 * TB * g)
                pool.tensor_copy(idx_next[:, :], tab[:, bass.ds(g * TB, TB), 0]).then_inc(idxn_rdy, 1)
                wait_apart(pool, idxn_rdy, g + 1)
                wait_apart(pool, st_done, DC * g)
                gather(xn_d, xn, idx_next, xs_ld)

            def scatter(g):
                for t in range(TB):
                    wait_apart(pool, ysum, TB * g + t + 1)
                    pool.indirect_dma_start(out, bass.IndirectOffsetOnAxis(ap=idx_cur[:, t:t + 1], axis=0), res[:, t, :], None,
                                            bounds_check=N - 1, oob_is_err=False).then_inc(out_st, 16)

            def bases(g):
                wait_apart(pool, out_st, 16 * TB * g)
                pool.tensor_copy(cur[:, :, :], tab[:, bass.ds(g * TB, TB), :]).then_inc(cur_rdy, 1)
                wait_apart(pool, cur_rdy, g + 1)
                pool.tensor_copy(idx_cur[:, :], cur[:, :, 0]).then_inc(idxc_rdy, 1)
                wait_apart(pool, idxc_rdy, g + 1)
                gather(base_d, res, idx_cur, bs_ld)

            pool.wait_ge(tab_ld, 16 * TB)
            pool.wait_ge(xn_st, 16 * B)
            pool.wait_ge(t_done, DC * B)
            tokens(0)
            pool.wait_ge(tab_ld2, 16 * (NT - TB))
            pool.wait_ge(base_st, 16 * B)

            def group(g, last):
                if not last:
                    tokens(g + 1)
                if not isinstance(g, int) or g:
                    scatter(g - 1)
                bases(g)

            rounds(pool, group, NG)
            scatter(NG - 1)
            pool.wait_ge(out_st, 16 * TB * NG)


def constants():
    P, D, N = 128, 256, 8192
    p = np.arange(P)
    ident = np.eye(P, dtype=np.float32)
    tri = (p[:, None] < p[None, :]).astype(np.float32)
    head = (p[:, None] // 16 == p[None, :] // 16).astype(np.float32)
    f = (np.arange(2)[None, :, None] * P + p[:, None, None]) // 16
    heads = (f == np.arange(16)[None, None, :]).astype(np.float32)
    spread = np.ascontiguousarray(heads.transpose(2, 1, 0))
    pairs = [(g, j, i) for g in range(2) for j in range(4) for i in range(4) if j < i]
    mask = np.zeros((4, 4), np.float32)
    row, ea, eb = (np.zeros(32, np.float32) for _ in range(3))
    for n, (g, j, i) in enumerate(pairs):
        mask[j, i] = 1
        slot = 16 * g + 4 * j + i
        row[slot], ea[slot], eb[slot] = n * N, (4 * g + j) * 4 * D, (4 * g + i) * 4 * D
    s = np.arange(32)
    before = (s[None, :] < s[:, None]).astype(np.float32)
    before = np.ascontiguousarray(np.broadcast_to(before, (P, 32, 32)))
    crow = np.concatenate([mask.ravel(), row, ea, eb])
    crow = np.ascontiguousarray(np.broadcast_to(crow, (P, crow.size)))
    part = np.stack([p * P, p] + [t * P + p for t in range(4)], 1).astype(np.float32)
    return {"c_ident": ident, "c_tri": tri, "c_head": head, "c_heads": heads, "c_spread": spread,
            "c_row": crow, "c_before": before, "c_part": part}


def kernel(**inputs):
    import concourse.bacc as bacc
    from concourse.bass_utils import run_bass_kernel_spmd

    a = {k: np.asarray(v) for k, v in inputs.items()}

    def chunks(w):
        k, n = w.shape
        return np.ascontiguousarray(w.reshape(k // 128, 128, n).transpose(1, 0, 2))

    def every(b):
        return np.ascontiguousarray(np.broadcast_to(b, (128, b.size)))

    w1 = chunks(a["L0_ffn_w1"].T).reshape(128, -1)
    w2 = np.ascontiguousarray(a["L0_ffn_w2"].transpose(0, 2, 1).reshape(8, 4, 128, 256).transpose(2, 0, 1, 3)).reshape(128, -1)
    arrays = {
        "x": a["L0_attn_inputs_q"],
        "w_kv": chunks(np.concatenate([a["L0_attn_Wk"], a["L0_attn_Wv"]], 1)),
        "w_q": chunks(a["L0_attn_Wq"]),
        "w_o": chunks(a["L0_attn_Wo"]),
        "w_in": chunks(a["L0_ffn_w_in"].T),
        "w_out": chunks(a["L0_ffn_w_out"].T),
        "w_exp": np.concatenate([w1, w2], 1),
        "w_rt": chunks(np.concatenate([a["L0_ffn_wg"], a["L0_ffn_we"]], 0).T),
        "b_q": np.ascontiguousarray(a["L0_attn_bq"].reshape(2, 128).T),
        "b_v": np.ascontiguousarray(a["L0_attn_bv"].reshape(2, 128).T),
        "b_k": every(a["L0_attn_bk"]),
        "b_o": every(a["L0_attn_bo"]),
        "b_rt": every(np.concatenate([a["L0_ffn_gb"], a["L0_ffn_eb"]])),
        **constants(),
    }
    arrays = {k: np.ascontiguousarray(v) for k, v in arrays.items()}
    nc = bacc.Bacc("TRN2", target_bir_lowering=False, num_devices=1)
    args = [nc.dram_tensor(k, v.shape, mybir.dt.from_np(v.dtype), kind="ExternalInput").ap() for k, v in arrays.items()]
    args.append(nc.dram_tensor("out", (8192, 256), mybir.dt.float32, kind="ExternalOutput").ap())
    layer_program(nc, *args)
    got = run_bass_kernel_spmd(nc, [arrays], core_ids=[0]).results[0]["out"]
    return got.reshape(16, 512, 256)
```

```python
import numpy as np
import concourse.bass as bass
from concourse import mybir
from contextlib import ExitStack


def layer_program(nc, x, w_kv, w_q, w_o, w_in, w_out, w_exp, w_rt, b_q, b_v, b_k, b_o, b_rt,
                  c_ident, c_tri, c_head, c_heads, c_spread, c_row, c_before, c_part, out):
    f32, f32r, bf16, i32 = mybir.dt.float32, mybir.dt.float32r, mybir.dt.bfloat16, mybir.dt.int32
    ALU = mybir.AluOpType
    ACT = mybir.ActivationFunctionType
    AX = mybir.AxisListType.X

    P = 128
    B, S, D = 16, 512, 256
    N = B * S
    TB = S // P
    DC = D // P
    HC = 4
    E = 8
    NCLS = 12
    NSLOT = 32
    NT = 76
    NG = NT // TB
    SENT = NCLS * N
    ROWS = SENT + P
    UNIT = (2 * 1024 + E * HC * D) // B
    EPS_LN, EPS_N = 1e-5, 1e-6

    xn_d = nc.dram_tensor("xn_d", (N + P, D), f32, kind="Internal").ap()
    base_d = nc.dram_tensor("base_d", (N + P, D), f32, kind="Internal").ap()
    tab_d = nc.dram_tensor("tab_d", (ROWS, 4), i32, kind="Internal").ap()

    ctx = ExitStack()
    with ctx:
        def sb(name, shape, dt):
            return ctx.enter_context(nc.sbuf_tensor(name, shape, dt))

        def sem(name):
            return ctx.enter_context(nc.semaphore(name))

        def pair(name, shape):
            return sb(name + "_hi", shape, f32r), sb(name + "_lo", shape, f32r)

        wkv_hi, wkv_lo = pair("wkv", [P, DC, 512])
        wq_hi, wq_lo = pair("wq", [P, DC, D])
        win_hi, win_lo = pair("win", [P, DC, 1024])
        wout_hi, wout_lo = pair("wout", [P, HC, D])
        wexp_hi, wexp_lo = pair("wexp", [P, B * UNIT])
        wo = sb("wo", [P, DC, D], f32)
        wrt = sb("wrt", [P, DC, 2, 10], f32r)
        wstage = sb("wstage", [P, UNIT], f32)

        xt = sb("xt", [P, TB, D], f32)
        res = sb("res", [P, TB, D], f32)
        xn = sb("xn", [P, TB, D], f32)
        xnT_hi, xnT_lo = pair("xnT", [P, DC, S])
        kb = sb("kb", [P, TB, D], f32)
        expt = sb("expt", [P, 2, 512], f32)
        relut = sb("relut", [P, 2, 512], f32)
        phik = sb("phik", [P, TB, D], f32)
        v = sb("v", [P, TB, D], f32)
        qn = v[:, :, :].rearrange("p t n -> p (t n)").rearrange("p (c s) -> p c s", c=DC)
        phiq = sb("phiq", [P, DC, S], f32)
        qn_hi, qn_lo = pair("qn", [P, DC, S])
        gated = sb("gated", [P, 2, S], f32)
        h_hi, h_lo = pair("h", [P, HC, S])
        m_hi, m_lo = pair("m", [P, DC, D])
        r16_hi, r16_lo = qn_hi[0:16, 1, :], qn_lo[0:16, 1, :]

        ident = sb("ident", [P, P], f32)
        triones = sb("triones", [P, 2, P], bf16)
        tri_f = relut[:, 0, 0:P]
        wrt_f = relut[:, 1, 384:384 + 10 * DC].rearrange("p (c n) -> p c n", c=DC)
        head = sb("head", [P, P], f32)
        heads = sb("heads", [P, DC, 16], f32)
        spread = sb("spread", [16, DC, P], f32r)
        spread_f = relut[0:16, 0, P:3 * P].rearrange("p (c n) -> p c n", c=DC)
        NROW = 16 + 3 * NSLOT
        crow = sb("crow", [P, NROW], f32)
        cpart = sb("cpart", [P, 6], f32)
        bq = sb("bq", [P, DC], f32)
        nbq = sb("nbq", [P, DC], f32)
        bv = sb("bv", [P, DC, P], f32)
        bk = sb("bk", [P, D], f32)
        bo = sb("bo", [P, D], f32)
        brt = sb("brt", [P, 10], f32)

        stats = sb("stats", [P, TB, 6], f32)
        mv = sb("mv", [P, TB, 2], f32)
        var = sb("var", [P, TB], f32)
        mhalf = sb("mhalf", [P, TB], f32)
        rstd = sb("rstd", [P, TB], f32)
        ksum = sb("ksum", [P, DC], f32)
        khead = sb("khead", [P, DC, 16], f32)
        kvm = relut[:, 0, 0:DC * P].rearrange("p (c n) -> p c n", c=DC)
        kvT = relut[:, 1, 0:DC * P].rearrange("p (c n) -> p c n", c=DC)
        onec = sb("onec", [P, 1], f32)
        rn = sb("rn", [P, TB, 16], f32)

        lg = sb("lg", [P, TB, 10], f32)
        lmax = sb("lmax", [P, TB, 3], f32)
        ex = sb("ex", [P, TB, 10], f32)
        gg = sb("gg", [P, TB, 2], f32)
        gsum = sb("gsum", [P, TB], f32)
        exs = sb("exs", [P, TB, 2, 4], f32)
        w4 = sb("w4", [P, TB, 4], f32)
        esum = sb("esum", [P, TB], f32)
        cmp = sb("cmp", [P, TB, 4, 4], f32)
        cmq = sb("cmq", [P, TB, 4, 4], f32)
        win = sb("win", [P, TB, 4], f32)
        oh = sb("oh", [P, TB, NSLOT], bf16)
        rank = sb("rank", [P, TB + 1, NSLOT], f32)
        run = sb("run", [P, NSLOT], f32)
        pos = sb("pos", [P, TB], f32)
        pos_i = sb("pos_i", [P, TB], i32)
        tok = sb("tok", [P, TB], f32)
        rows = sb("rows", [P, TB, 4], i32)
        fill = relut[:, 1, 0:4 * N // P].bitcast(i32).rearrange("p (n w) -> p n w", w=4)
        cnt = sb("cnt", [P, NSLOT], f32)
        cnt_i = sb("cnt_i", [P, NSLOT], i32)
        first = sb("first", [P, NSLOT], f32)
        memb = sb("memb", [P, NSLOT], f32)
        memt = relut[:, 1, 256:256 + 3 * NSLOT].rearrange("p (n c) -> p n c", n=3)
        info = sb("info", [P, 4], f32)
        info_i = sb("info_i", [1, 3, NT], i32)
        tab = phik[:, :, :].rearrange("p t d -> p (t d)")[:, 0:4 * NT].bitcast(i32).rearrange("p (n w) -> p n w", w=4)
        idx_next = sb("idx_next", [P, TB], i32)
        cur = sb("cur", [P, TB, 4], i32)
        idx_cur = sb("idx_cur", [P, TB], i32)

        pair_mask = crow[:, 0:16]
        slot_row = crow[:, 16:16 + NSLOT]
        slot_ea = crow[:, 16 + NSLOT:16 + 2 * NSLOT]
        slot_eb = crow[:, 16 + 2 * NSLOT:16 + 3 * NSLOT]
        before = xt[:, :, :].rearrange("p t d -> p (t d)").rearrange("p (a c) -> p a c", a=NSLOT)
        part128 = cpart[:, 0:1]
        part = cpart[:, 1:2]
        tok0 = cpart[:, 2:6]

        bank = [ctx.enter_context(nc.psum_tensor(f"bank{i}", [P, 512], f32)) for i in range(8)]

        setup_ld = sem("setup_ld")
        x_ld = sem("x_ld")
        w_ld = sem("w_ld")
        xn_st = sem("xn_st")
        base_st = sem("base_st")
        fill_st = sem("fill_st")
        w_split = sem("w_split")
        w_round = sem("w_round")
        fill_set = sem("fill_set")
        const_set = sem("const_set")
        passed = sem("passed")
        v_link = sem("v_link")
        g_link = sem("g_link")
        wexp_split = sem("wexp_split")
        t_done = sem("t_done")
        l_done = sem("l_done")
        kv_done = sem("kv_done")
        q_done = sem("q_done")
        hid_done = sem("hid_done")
        acc_done = sem("acc_done")
        rt_done = sem("rt_done")
        kvt_done = sem("kvt_done")
        nb_done = sem("nb_done")
        m_done = sem("m_done")
        y_done = sem("y_done")
        info_done = sem("info_done")
        thi = sem("thi")
        v_rdy = sem("v_rdy")
        ek_rdy = sem("ek_rdy")
        eq_rdy = sem("eq_rdy")
        ex_rdy = sem("ex_rdy")
        neg_rdy = sem("neg_rdy")
        sil_rdy = sem("sil_rdy")
        hhi_rdy = sem("hhi_rdy")
        rhi_rdy = sem("rhi_rdy")
        qhi_rdy = sem("qhi_rdy")
        mhi_rdy = sem("mhi_rdy")
        xn_rdy = sem("xn_rdy")
        tlo = sem("tlo")
        kb_rdy = sem("kb_rdy")
        phik_rdy = sem("phik_rdy")
        phiq_rdy = sem("phiq_rdy")
        lg_rdy = sem("lg_rdy")
        oh_rdy = sem("oh_rdy")
        gate_rdy = sem("gate_rdy")
        kvm_rdy = sem("kvm_rdy")
        var_rdy = sem("var_rdy")
        rank_rd = sem("rank_rd")
        kvT_rdy = sem("kvT_rdy")
        row_rdy = sem("row_rdy")
        rn_rdy = sem("rn_rdy")
        rlo_rdy = sem("rlo_rdy")
        qn_rdy = sem("qn_rdy")
        qlo_rdy = sem("qlo_rdy")
        mlo_rdy = sem("mlo_rdy")
        base_rdy = sem("base_rdy")
        info_rdy = sem("info_rdy")
        kstep0 = sem("kstep0")
        kstep = sem("kstep")
        t_link = sem("t_link")
        ystep = sem("ystep")
        infoi_rdy = sem("infoi_rdy")
        rstd_rdy = sem("rstd_rdy")
        res_rdy = sem("res_rdy")
        hlo_rdy = sem("hlo_rdy")
        row_st = sem("row_st")
        tab_ld = sem("tab_ld")
        xs_ld = sem("xs_ld")
        bs_ld = sem("bs_ld")
        out_st = sem("out_st")
        idxn_rdy = sem("idxn_rdy")
        idxc_rdy = sem("idxc_rdy")
        cur_rdy = sem("cur_rdy")
        st_done = sem("st_done")
        shid_done = sem("shid_done")
        sw_done = sem("sw_done")
        sthi = sem("sthi")
        stlo = sem("stlo")
        ssil = sem("ssil")
        sgate = sem("sgate")
        shhi = sem("shhi")
        shlo = sem("shlo")
        ysum = sem("ysum")

        block = ctx.enter_context(nc.Block())

        def wait(e, s, n):
            if not isinstance(n, int) or n > 0:
                e.wait_ge(s, n)

        def wait_apart(e, s, n):
            wait(e, s, n)
            if not isinstance(n, int):
                e.sem_inc(passed, 1)

        def rounds(e, body, n):
            body(0, False)
            with e.Fori(1, n - 1) as i:
                body(i, False)
            body(n - 1, True)

        stage = [
            (kb[:, :, :].rearrange("p t n -> p (t n)"), w_kv, wkv_hi, wkv_lo, "p c n -> p (c n)"),
            (v[:, 0:2, :].rearrange("p t n -> p (t n)"), w_q, wq_hi, wq_lo, "p c n -> p (c n)"),
            (phik[:, :, :].rearrange("p t n -> p (t n)"), w_in[:, 0, :], win_hi[:, 0, :], win_lo[:, 0, :], None),
            (phiq[:, :, :].rearrange("p t n -> p (t n)"), w_in[:, 1, :], win_hi[:, 1, :], win_lo[:, 1, :], None),
            (gated[:, :, :].rearrange("p t n -> p (t n)"), w_out, wout_hi, wout_lo, "p c n -> p (c n)"),
        ]

        def x_rows(b):
            return x[bass.ds(b, 1), :, :].rearrange("o (t p) d -> p (o t) d", p=P)

        def rows_of(d, b):
            return d[bass.ds(b * S, S), :].rearrange("(t p) d -> p t d", p=P)

        zero_rows = wexp_lo[:, 0:D].bitcast(f32)

        def mm3(e, to, w_hi, w_lo, m_hi_, m_lo_, first_, last_, free=False):
            e.matmul(to, w_hi, m_hi_, start=first_, stop=False, skip_group_check=free)
            e.matmul(to, w_hi, m_lo_, start=False, stop=False, skip_group_check=free)
            return e.matmul(to, w_lo, m_hi_, start=False, stop=last_, skip_group_check=free)

        @block.sync
        def _(sp):
            sp.dma_start(xt[:, :, :], x[0, :, :].rearrange("(t p) d -> p t d", p=P)).then_inc(x_ld, 16)
            for to, of in ((ident[:], c_ident), (tri_f, c_tri), (head[:], c_head), (heads[:], c_heads), (spread_f, c_spread),
                           (crow[:], c_row), (cpart[:], c_part), (bq[:], b_q), (bv[:, :, :].rearrange("p c n -> p (c n)"), b_v), (bk[:], b_k), (bo[:], b_o), (brt[:], b_rt),
                           (wo[:], w_o), (wrt_f, w_rt)):
                sp.dma_start(to, of).then_inc(setup_ld, 16)
            for buf, of, _, _, flat in stage:
                sp.dma_start(buf, of.rearrange(flat) if flat else of).then_inc(setup_ld, 16)
            sp.wait_ge(fill_set, 3)
            for c in range(NCLS):
                sp.dma_start(tab_d[c * N:(c + 1) * N, :].rearrange("(p n) w -> p n w", p=P), fill[:, :, :]).then_inc(fill_st, 16)
            sp.dma_start(tab_d[SENT:ROWS, :], fill[:, 0, :]).then_inc(fill_st, 16)
            sp.dma_start(xn_d[N:N + P, :], zero_rows).then_inc(fill_st, 16)
            sp.dma_start(base_d[N:N + P, :], zero_rows).then_inc(fill_st, 16)

            def load_store(b, last):
                wait(sp, wexp_split, b)
                sp.dma_start(wstage[:, :], w_exp[:, bass.ds(b * UNIT, UNIT)]).then_inc(w_ld, 16)
                if not last:
                    sp.wait_ge(res_rdy, b + 1)
                    sp.wait_ge(xn_rdy, b + 1)
                    sp.dma_start(xt[:, :, :], x_rows(b + 1)).then_inc(x_ld, 16)
                    sp.wait_ge(xn_rdy, b + 2)
                    sp.dma_start(rows_of(xn_d, b + 1), xn[:, :, :]).then_inc(xn_st, 16)
                else:
                    sp.wait_ge(res_rdy, B)
                    sp.dma_start(before, c_before).then_inc(x_ld, 16)
                sp.wait_ge(base_rdy, DC * (b + 1))
                sp.dma_start(rows_of(base_d, b), res[:, :, :]).then_inc(base_st, 16)

            sp.wait_ge(xn_rdy, 1)
            sp.dma_start(rows_of(xn_d, 0), xn[:, :, :]).then_inc(xn_st, 16)
            rounds(sp, load_store, B)

            sp.wait_ge(infoi_rdy, 1)
            sp.wait_ge(row_st, 16 * TB * B)
            sp.wait_ge(fill_st, 16 * (NCLS + 3))
            def tables(g):
                wait_apart(sp, tab_ld, 16 * TB * g)
                for t in range(TB):
                    at = sp.value_load(info_i[0:1, 2, bass.ds(g * TB + t, 1)], min_val=0, max_val=SENT)
                    sp.dma_start(tab[:, bass.ds(g * TB + t, 1), :].rearrange("p t w -> p (t w)"),
                                 tab_d[bass.ds(at, P), :]).then_inc(tab_ld, 16)
            tables(0)
            with sp.Fori(1, NG) as g:
                tables(g)
            sp.wait_ge(xn_st, 16 * B)
            sp.wait_ge(base_st, 16 * B)

        @block.tensor
        def _(pe):
            def transposes(banks, done, free_sem, free_of, ready, ready_n):
                pe.wait_ge(ready, ready_n)
                for c in range(DC):
                    wait(pe, free_sem[c], free_of[c])
                    for t in range(TB):
                        mm = pe.transpose(bank[banks[c]][:, t * P:(t + 1) * P], xn[:, t, c * P:(c + 1) * P], ident[:, :])
                    mm.then_inc(done, 1)

            def logits(t, k):
                c, src = k // 2, (xnT_hi, xnT_lo)[k % 2]
                return pe.matmul(bank[7][:, 20 * t:20 * t + 20], src[:, c, t * P:(t + 1) * P],
                                 wrt[:, c, :, :].rearrange("p a n -> p (a n)"), start=(k == 0), stop=(k == 3))

            def normaliser(k):
                t, c = k // DC, k % DC
                return pe.matmul(bank[6][:, 16 * t:16 * t + 16], phiq[:, c, t * P:(t + 1) * P], khead[:, c, :],
                                 start=(c == 0), stop=(c == DC - 1))

            def hidden(j, banks, frees, w_hi, w_lo, done, beside=None):
                for half in range(2):
                    if half == 0:
                        wait(pe, frees[0][0], frees[0][1])
                    else:
                        wait(pe, frees[1][0], frees[1][1])
                    lo = half * 512 + j * P
                    for c in range(DC):
                        mm = mm3(pe, bank[banks[half]][:, :], w_hi[:, c, lo:lo + P], w_lo[:, c, lo:lo + P],
                                 xnT_hi[:, c, :], xnT_lo[:, c, :], c == 0, c == DC - 1)
                        if beside is not None:
                            for k in range(2):
                                small = beside(4 * half + 2 * c + k)
                if beside is not None:
                    small.then_inc(nb_done, 1)
                mm.then_inc(done, 1)

            def batch(b, last):
                for t in range(TB):
                    if t == 0:
                        pe.wait_ge(tlo, DC * (b + 1))
                        wait(pe, sil_rdy, HC * b)
                        wait(pe, qn_rdy, DC * b)
                    elif t == 1:
                        wait(pe, gate_rdy, HC * b)
                    for c in range(DC):
                        mm = mm3(pe, bank[t][:, :], xnT_hi[:, c, t * P:(t + 1) * P], xnT_lo[:, c, t * P:(t + 1) * P],
                                 wkv_hi[:, c, :], wkv_lo[:, c, :], c == 0, c == DC - 1)
                        if c == 0:
                            logits(t, 0)
                            logits(t, 1)
                        else:
                            logits(t, 2)
                            lg_mm = logits(t, 3)
                    mm.then_inc(kv_done, 1)
                lg_mm.then_inc(l_done, 1)
                for o in range(DC):
                    if o == 0:
                        wait(pe, mlo_rdy, b)
                    else:
                        wait(pe, base_rdy, DC * b - 1)
                    for c in range(DC):
                        mm = mm3(pe, bank[4 + o][:, :], wq_hi[:, c, o * P:(o + 1) * P], wq_lo[:, c, o * P:(o + 1) * P],
                                 xnT_hi[:, c, :], xnT_lo[:, c, :], c == 0, c == DC - 1)
                    mm.then_inc(q_done, 1)
                hidden(0, (6, 7), ((base_rdy, DC * b), (lg_rdy, b + 1)), win_hi, win_lo, hid_done)
                pe.wait_ge(phik_rdy, 2 * (b + 1))
                pe.wait_ge(v_rdy, TB * (b + 1))
                for c in range(DC):
                    for t in range(TB):
                        pe.matmul(bank[2][:, c * P:(c + 1) * P], phik[:, t, c * P:(c + 1) * P], v[:, t, c * P:(c + 1) * P],
                                  start=(c == 0 and t == 0), stop=(t == TB - 1), skip_group_check=True)
                        mm = pe.matmul(bank[2][:, 256 + c:257 + c], phik[:, t, c * P:(c + 1) * P], onec[:, :],
                                       start=False, stop=(t == TB - 1), skip_group_check=True)
                mm.then_inc(acc_done, 1)
                hidden(1, (0, 1), ((v_rdy, TB * b + 1), (v_rdy, TB * b + 2)), win_hi, win_lo, hid_done)
                pe.wait_ge(kvm_rdy, b + 1)
                pe.wait_ge(eq_rdy, DC * (b + 1))
                for c in range(DC):
                    mm = pe.transpose(bank[5][:, c * P:(c + 1) * P], kvm[:, c, :], ident[:, :])
                mm.then_inc(kvt_done, 1)
                pe.wait_ge(phiq_rdy, DC * (b + 1))
                pe.wait_ge(gate_rdy, HC * b + 1)
                hidden(2, (3, 4), ((v_rdy, TB * (b + 1)), (eq_rdy, DC * b + 1)), win_hi, win_lo, hid_done, normaliser)
                hidden(3, (0, 1), ((sil_rdy, HC * b + 2), (gate_rdy, HC * b + 2)), win_hi, win_lo, hid_done)
                pe.wait_ge(rn_rdy, b + 1)
                for t in range(TB):
                    mm = pe.transpose(bank[7][0:16, t * P:(t + 1) * P], rn[:, t, :], ident[:, :])
                mm.then_inc(nb_done, 1)
                pe.wait_ge(oh_rdy, b + 1)
                pe.wait_ge(kvT_rdy, b + 1)
                W = NSLOT
                pe.matmul(bank[5][:, 256:256 + TB * W], triones[:, 0, :], oh[:, :, :].rearrange("p t c -> p (t c)"),
                          start=True, stop=False, skip_group_check=True)
                for n in range(TB, 0, -1):
                    o = 256 + (TB + 1 - n) * W
                    mm = pe.matmul(bank[5][:, o:o + n * W], triones[:, 1, :], oh[:, 0:n, :].rearrange("p t c -> p (t c)"),
                                   start=False, stop=(n == 1), skip_group_check=True)
                mm.then_inc(rt_done, 1)
                pe.wait_ge(gate_rdy, HC * b + 3)
                for c in range(DC):
                    mm = pe.matmul(bank[4][:, c * D:(c + 1) * D], kvT[:, c, :], wo[:, c, :], start=True, stop=True)
                mm.then_inc(m_done, 1)
                if not last:
                    transposes((2, 3), t_done, (kvm_rdy, sil_rdy), (b + 1, HC * b + 3), xn_rdy, b + 2)
                else:
                    pe.wait_ge(info_rdy, 1)
                    for n in range(3):
                        mm = pe.matmul(bank[2][0:1, n * NT:(n + 1) * NT], info[0:NT, n:n + 1], ident[0:NT, 0:NT],
                                       start=True, stop=True)
                    mm.then_inc(info_done, 1)
                pe.wait_ge(rlo_rdy, b + 1)
                for c in range(DC):
                    pe.matmul(bank[6 + c][:, :], spread[:, c, :], r16_hi, start=True, stop=False)
                    mm = pe.matmul(bank[6 + c][:, :], spread[:, c, :], r16_lo, start=False, stop=True)
                    mm.then_inc(nb_done, 1)
                def y(t):
                    return bank[5 + t // 2][:, (t % 2) * D:(t % 2 + 1) * D]
                pe.wait_ge(rank_rd, b + 1)
                pe.wait_ge(hlo_rdy, HC * b + 3)
                for t in range(TB):
                    if t == 2:
                        pe.wait_ge(qn_rdy, DC * b + 1)
                    for j in range(HC - 1):
                        mm3(pe, y(t), h_hi[:, j, t * P:(t + 1) * P], h_lo[:, j, t * P:(t + 1) * P],
                            wout_hi[:, j, :], wout_lo[:, j, :], t % 2 == 0 and j == 0, False, True)
                pe.wait_ge(mlo_rdy, b + 1)
                pe.wait_ge(qlo_rdy, DC * (b + 1))
                for t in range(TB):
                    for c in range(DC):
                        mm3(pe, y(t), qn_hi[:, c, t * P:(t + 1) * P], qn_lo[:, c, t * P:(t + 1) * P],
                            m_hi[:, c, :], m_lo[:, c, :], False, False, True)
                pe.wait_ge(hlo_rdy, HC * (b + 1))
                for t in range(TB):
                    mm = mm3(pe, y(t), h_hi[:, 3, t * P:(t + 1) * P], h_lo[:, 3, t * P:(t + 1) * P],
                             wout_hi[:, 3, :], wout_lo[:, 3, :], False, True, True)
                    if t % 2 == 1:
                        mm.then_inc(y_done, 1)

            pe.wait_ge(const_set, 3)
            pe.wait_ge(setup_ld, 16 * (14 + len(stage)))
            transposes((2, 3), t_done, (t_done, t_done), (0, 0), xn_rdy, 1)
            pe.wait_ge(w_split, 1)
            pe.wait_ge(kstep0, 2)
            rounds(pe, batch, B)

            w1_hi = wexp_hi[:, 0:2048].rearrange("p (c n) -> p c n", c=DC)
            w1_lo = wexp_lo[:, 0:2048].rearrange("p (c n) -> p c n", c=DC)
            pe.wait_ge(wexp_split, B)
            pe.wait_ge(infoi_rdy, 1)
            pe.wait_ge(tlo, DC * B)
            transposes((1, 2), st_done, (gate_rdy, infoi_rdy), (HC * B, 1), xs_ld, 16 * TB)

            def group(g, last):
                pe.wait_ge(stlo, DC * (g + 1))

                def experts(t):
                    return [pe.value_load(info_i[0:1, n, bass.ds(g * TB + t, 1)], min_val=0, max_val=(E - 1) * HC * D)
                            for n in range(2)]
                hidden(0, (0, 1), ((sgate, HC * g), (stlo, DC * g + 1)), w1_hi, w1_lo, shid_done)
                at = [experts(0)]
                hidden(1, (2, 3), ((stlo, DC * (g + 1)), (ysum, TB * g - 3)), w1_hi, w1_lo, shid_done)
                at.append(experts(1))
                if isinstance(g, int) and g == 0:
                    pe.wait_ge(base_rdy, DC * B)
                hidden(2, (4, 5), ((ysum, TB * g - 2), (ysum, TB * g - 1)), w1_hi, w1_lo, shid_done)
                at.append(experts(2))
                hidden(3, (6, 0), ((ysum, TB * g), (ssil, HC * g + 1)), w1_hi, w1_lo, shid_done)
                at.append(experts(3))
                if not last:
                    transposes((1, 2), st_done, (sgate, ssil), (HC * g + 1, HC * g + 2), xs_ld, 16 * TB * (g + 2))
                free = ((sgate, HC * g + 2), (ssil, HC * g + 3), (sgate, HC * g + 3), (ssil, HC * g + 4))

                def second(t, js, start, stop):
                    for n in range(2):
                        for j in js:
                            off = at[t][n] + (2048 + j * D)
                            r_hi = wexp_hi[:, bass.ds(off, D)]
                            r_lo = wexp_lo[:, bass.ds(off, D)]
                            mm = mm3(pe, bank[3 + t][:, n * D:(n + 1) * D], h_hi[:, j, t * P:(t + 1) * P],
                                     h_lo[:, j, t * P:(t + 1) * P], r_hi, r_lo, start and n == 0 and j == 0, stop, True)
                    return mm
                pe.wait_ge(shlo, HC * g + 3)
                for t in range(TB):
                    pe.wait_ge(*free[t])
                    second(t, range(HC - 1), True, False)
                pe.wait_ge(shlo, HC * (g + 1))
                for t in range(TB):
                    second(t, (HC - 1,), False, True).then_inc(sw_done, 1)

            rounds(pe, group, NG)

        @block.scalar
        def _(act):
            act.wait_ge(setup_ld, 16 * (14 + len(stage)))
            for buf, _, hi, _, flat in stage:
                act.copy(hi[:].rearrange(flat) if flat else hi, buf).then_inc(w_round, 1)

            def t_high(b):
                for c in range(DC):
                    act.wait_ge(t_done, DC * b + c + 1)
                    wait(act, hid_done, HC * b)
                    act.copy(xnT_hi[:, c, :], bank[2 + c][:, :]).then_inc(thi, 1)

            def silu(j, n, hid, gate_bank, lo_prev, sil, first_wait=None):
                act.wait_ge(hid, n + 1)
                wait(act, lo_prev, n - 1)
                act.activation(gated[:, j % 2, :], bank[gate_bank][:, :], ACT.Silu).then_inc(sil, 1)

            def high(j, n, gate, hhi):
                act.wait_ge(gate, n + 1)
                act.copy(h_hi[:, j, :], gated[:, j % 2, :]).then_inc(hhi, 1)

            def batch(b, last):
                for t in range(TB):
                    act.wait_ge(kb_rdy, TB * b + t + 1)
                    wait(act, qlo_rdy, DC * b)
                    act.copy(v[:, t, :], bank[t][:, D:2 * D]).then_inc(v_rdy, 1)
                    if t % 2 == 1:
                        i = t // 2
                        wait(act, phiq_rdy, DC * (b - 1) + i + 1)
                        src = kb[:, 2 * i:2 * i + 2, :].rearrange("p t n -> p (t n)")
                        act.activation(expt[:, i, :], src, ACT.Relu, scale=-1.0).then_inc(neg_rdy, 1)
                        act.wait_ge(neg_rdy, 4 * b + i + 1)
                        act.activation(expt[:, i, :], expt[:, i, :], ACT.Exp, scale=-1.0).then_inc(ek_rdy, 1)
                for o in range(DC):
                    act.wait_ge(q_done, DC * b + o + 1)
                    act.wait_ge(phik_rdy, 2 * b + o + 1)
                    act.activation(expt[:, o, :], bank[4 + o][:, :], ACT.Relu, bias=nbq[:, o:o + 1], scale=-1.0).then_inc(neg_rdy, 1)
                    act.activation(relut[:, o, :], bank[4 + o][:, :], ACT.Relu, bias=bq[:, o:o + 1])
                    act.wait_ge(neg_rdy, 4 * b + o + 3)
                    act.activation(expt[:, o, :], expt[:, o, :], ACT.Exp, scale=-1.0).then_inc(eq_rdy, 1)
                act.wait_ge(lg_rdy, b + 1)
                act.activation(ex[:, :, :], lg[:, :, :], ACT.Exp).then_inc(ex_rdy, 1)
                wait(act, y_done, DC * b)
                gates = (6, 0, 3, 0)
                for j in range(HC):
                    silu(j, HC * b + j, hid_done, gates[j], hlo_rdy, sil_rdy)
                    if j == 3:
                        act.wait_ge(nb_done, 4 * b + 2)
                        act.copy(r16_hi, bank[7][0:16, :]).then_inc(rhi_rdy, 1)
                        act.wait_ge(m_done, b + 1)
                        act.copy(m_hi[:, :, :].rearrange("p c n -> p (c n)"), bank[4][:, :]).then_inc(mhi_rdy, 1)
                    high(j, HC * b + j, gate_rdy, hhi_rdy)
                    if j == 1:
                        act.wait_ge(kvt_done, b + 1)
                        act.copy(kvT[:, :, :].rearrange("p c n -> p (c n)"), bank[5][:, 0:DC * P]).then_inc(kvT_rdy, 1)
                if not last:
                    t_high(b + 1)
                for c in range(DC):
                    act.wait_ge(qn_rdy, DC * b + c + 1)
                    act.copy(qn_hi[:, c, :], qn[:, c, :]).then_inc(qhi_rdy, 1)

            t_high(0)
            act.wait_ge(fill_st, 16 * (NCLS + 3))
            rounds(act, batch, B)

            def st_high(g):
                for c in range(DC):
                    act.wait_ge(st_done, DC * g + c + 1)
                    wait(act, shid_done, HC * g)
                    act.copy(xnT_hi[:, c, :], bank[1 + c][:, :]).then_inc(sthi, 1)

            def group(g, last):
                gates = (0, 2, 4, 6)
                wait(act, sw_done, TB * g)
                for j in range(HC):
                    silu(j, HC * g + j, shid_done, gates[j], shlo, ssil)
                    high(j, HC * g + j, sgate, shhi)
                if not last:
                    st_high(g + 1)

            act.wait_ge(hid_done, HC * B)
            act.wait_ge(y_done, DC * B)
            act.wait_ge(hlo_rdy, HC * B)
            st_high(0)
            rounds(act, group, NG)

        @block.vector
        def _(dve):
            LN_LINKS, RT_LINKS, RK_LINKS = 2, 27, 3
            PER = LN_LINKS + RT_LINKS + RK_LINKS
            state = [0, 0]

            def start(n):
                state[:] = n, 0

            def link(ins):
                ins.then_inc(v_link, 1)
                state[1] += 1
                dve.wait_ge(v_link, state[0] + state[1])

            def norm(b):
                dve.wait_ge(x_ld, 16 * (b + 1))
                for t in range(TB):
                    ins = dve.bn_stats(stats[:, t, :], xt[:, t, :])
                link(ins)
                if not isinstance(b, int):
                    dve.sem_inc(passed, 1)
                for t in range(TB):
                    ins = dve.bn_aggr(mv[:, t, :], stats[:, t, :])
                link(ins)
                dve.tensor_scalar(var[:, :], mv[:, :, 1], EPS_LN, None, ALU.add).then_inc(var_rdy, 1)

            def normalise(b):
                dve.wait_ge(rstd_rdy, b + 1)
                wait(dve, xn_st, 16 * b)
                wait(dve, t_done, DC * b)
                for t in range(TB):
                    ins = dve.tensor_scalar(xn[:, t, :], xt[:, t, :], mv[:, t, 0:1], rstd[:, t:t + 1], ALU.subtract, ALU.mult)
                ins.then_inc(xn_rdy, 1)

            def t_low(b):
                for c in range(DC):
                    dve.wait_ge(thi, DC * b + c + 1)
                    dve.tensor_tensor(xnT_lo[:, c, :], bank[2 + c][:, :], xnT_hi[:, c, :].bitcast(f32), ALU.subtract).then_inc(tlo, 1)

            def logits_in(b):
                dve.wait_ge(l_done, b + 1)
                both = bank[7][:, 0:20 * TB].rearrange("p (t a n) -> p t a n", t=TB, a=2)
                link(dve.tensor_tensor(lg[:, :, :], both[:, :, 0, :], brt[:, :].unsqueeze(1).broadcast_to([P, TB, 10]), ALU.add))
                link(dve.tensor_tensor(lg[:, :, :], both[:, :, 1, :], lg[:, :, :], ALU.add))
                link(dve.tensor_tensor(lmax[:, :, 0], lg[:, :, 0], lg[:, :, 1], ALU.max))
                link(dve.tensor_reduce(lmax[:, :, 1:3], lg[:, :, 2:10].rearrange("p t (g e) -> p t g e", g=2), AX, ALU.max))
                dve.tensor_tensor(lg[:, :, 0:2], lg[:, :, 0:2], lmax[:, :, 0:1].broadcast_to([P, TB, 2]), ALU.subtract)
                l8 = lg[:, :, 2:10].rearrange("p t (g e) -> p t g e", g=2)
                dve.tensor_tensor(l8, l8, lmax[:, :, 1:3].unsqueeze(3).broadcast_to([P, TB, 2, 4]), ALU.subtract).then_inc(lg_rdy, 1)

            wj = w4[:, :, :].unsqueeze(3).broadcast_to([P, TB, 4, 4])
            wi = w4[:, :, :].unsqueeze(2).broadcast_to([P, TB, 4, 4])

            def probabilities(b):
                dve.wait_ge(ex_rdy, b + 1)
                link(dve.tensor_tensor(gg[:, :, 1], ex[:, :, 1], ex[:, :, 0], ALU.is_gt))
                link(dve.tensor_scalar(gg[:, :, 0], gg[:, :, 1], -1.0, 1.0, ALU.mult, ALU.add))
                link(dve.tensor_tensor(gsum[:, :], ex[:, :, 0], ex[:, :, 1], ALU.add))
                g4 = gg[:, :, :].unsqueeze(3).broadcast_to([P, TB, 2, 4])
                link(dve.tensor_tensor(exs[:, :, :, :], ex[:, :, 2:10].rearrange("p t (g e) -> p t g e", g=2), g4, ALU.mult))
                link(dve.tensor_tensor(w4[:, :, :], exs[:, :, 0, :], exs[:, :, 1, :], ALU.add))
                link(dve.tensor_reduce(esum[:, :], w4[:, :, :], AX, ALU.add))
                link(dve.tensor_tensor(esum[:, :], esum[:, :], gsum[:, :], ALU.mult))
                link(dve.reciprocal(gsum[:, :], esum[:, :]))
                link(dve.tensor_tensor(w4[:, :, :], w4[:, :, :], gsum[:, :].unsqueeze(2).broadcast_to([P, TB, 4]), ALU.mult))

            def best_two(b):
                msk = pair_mask.rearrange("p (j i) -> p j i", j=4).unsqueeze(1).broadcast_to([P, TB, 4, 4])
                link(dve.tensor_tensor(cmp[:, :, :, :], wj, wi, ALU.is_gt))
                link(dve.tensor_tensor(cmq[:, :, :, :], wj, wi, ALU.is_equal))
                link(dve.tensor_tensor(cmq[:, :, :, :], cmq[:, :, :, :], msk, ALU.mult))
                link(dve.tensor_tensor(cmp[:, :, :, :], cmp[:, :, :, :], cmq[:, :, :, :], ALU.add))
                link(dve.tensor_reduce(win[:, :, :], cmp[:, :, :, :], AX, ALU.add))
                link(dve.tensor_scalar(win[:, :, :], win[:, :, :], 2.0, None, ALU.is_ge))
                link(dve.tensor_tensor(cmp[:, :, :, :], win[:, :, :].unsqueeze(3).broadcast_to([P, TB, 4, 4]),
                                       win[:, :, :].unsqueeze(2).broadcast_to([P, TB, 4, 4]), ALU.mult))
                link(dve.tensor_tensor(cmp[:, :, :, :], cmp[:, :, :, :], msk, ALU.mult))
                pr = cmp[:, :, :, :].rearrange("p t j i -> p t (j i)")
                for g in range(2):
                    ins = dve.tensor_tensor(oh[:, :, 16 * g:16 * g + 16], pr, gg[:, :, g:g + 1].broadcast_to([P, TB, 16]), ALU.mult)
                ins.then_inc(oh_rdy, 1)

            def table_rows(b):
                wait(dve, row_st, 16 * TB * b)
                wts = rows[:, :, :].bitcast(f32)
                q = cmq[:, :, :, :].rearrange("p t j i -> p t (j i)")
                link(dve.tensor_tensor(cmq[:, :, :, :], cmp[:, :, :, :], wj, ALU.mult))
                link(dve.tensor_reduce(wts[:, :, 1], q, AX, ALU.add))
                link(dve.tensor_tensor(cmq[:, :, :, :], cmp[:, :, :, :], wi, ALU.mult))
                link(dve.tensor_reduce(wts[:, :, 2], q, AX, ALU.add))
                link(dve.tensor_copy(rows[:, :, 0], tok[:, :]))
                link(dve.tensor_scalar(tok[:, :], tok[:, :], float(S), None, ALU.add))

            rank_bank = bank[5][:, 256:256 + 5 * NSLOT].rearrange("p (t c) -> p t c", c=NSLOT)

            def ranks_in(b):
                dve.wait_ge(rt_done, b + 1)
                dve.tensor_tensor(rank[:, :, :], rank_bank, run[:, :].unsqueeze(1).broadcast_to([P, TB + 1, NSLOT]),
                                  ALU.add).then_inc(rank_rd, 1)

            def ranks(b):
                dve.wait_ge(rank_rd, b + 1)
                link(dve.tensor_copy(run[:, :], rank[:, TB, :]))
                link(dve.tensor_tensor(rank[:, 0:TB, :], rank[:, 0:TB, :], oh[:, :, :], ALU.mult))
                link(dve.tensor_reduce(pos[:, :], rank[:, 0:TB, :], AX, ALU.add))
                dve.tensor_copy(pos_i[:, :], pos[:, :]).then_inc(row_rdy, 1)

            def gate(j, n, hid, up_bank, sil, out_sem):
                dve.wait_ge(sil, n + 1)
                dve.tensor_tensor(gated[:, j % 2, :], gated[:, j % 2, :], bank[up_bank][:, :], ALU.mult).then_inc(out_sem, 1)

            def batch(b, last):
                start(LN_LINKS + PER * b)

                def k_in(t):
                    dve.wait_ge(kv_done, TB * b + t + 1)
                    wait(dve, ek_rdy, 2 * b)
                    dve.tensor_tensor(kb[:, t, :], bank[t][:, 0:D], bk[:, :], ALU.add).then_inc(kb_rdy, 1)

                def phi_k(i):
                    dve.wait_ge(ek_rdy, 2 * b + i + 1)
                    wait(dve, acc_done, b)
                    dve.scalar_tensor_tensor(phik[:, 2 * i:2 * i + 2, :].rearrange("p t n -> p (t n)"),
                                             kb[:, 2 * i:2 * i + 2, :].rearrange("p t n -> p (t n)"), 0.0,
                                             expt[:, i, :], ALU.max, ALU.add).then_inc(phik_rdy, 1)

                for t in range(TB):
                    k_in(t)
                phi_k(0)
                logits_in(b)
                phi_k(1)
                for o in range(DC):
                    dve.wait_ge(eq_rdy, DC * b + o + 1)
                    wait(dve, nb_done, 4 * (b - 1) + 1)
                    dve.tensor_tensor(phiq[:, o, :], expt[:, o, :], relut[:, o, :], ALU.add).then_inc(phiq_rdy, 1)
                probabilities(b)
                gate(0, HC * b, hid_done, 7, sil_rdy, gate_rdy)
                dve.wait_ge(acc_done, b + 1)
                dve.tensor_copy(ksum[:, :], bank[2][:, 256:258]).then_inc(kstep, 1)
                dve.wait_ge(kstep, 3 * b + 1)
                for c in range(DC):
                    dve.tensor_scalar(khead[:, c, :], heads[:, c, :], ksum[:, c:c + 1], None, ALU.mult)
                for c in range(DC):
                    ins = dve.scalar_tensor_tensor(kvm[:, c, :], bv[:, c, :], ksum[:, c:c + 1], bank[2][:, c * P:(c + 1) * P],
                                                   ALU.mult, ALU.add)
                ins.then_inc(kstep, 1)
                dve.wait_ge(kstep, 3 * b + 2)
                dve.tensor_tensor(kvm[:, :, :], kvm[:, :, :], head[:, :].unsqueeze(1).broadcast_to([P, DC, P]),
                                  ALU.mult).then_inc(kvm_rdy, 1)
                wait(dve, rt_done, b)
                best_two(b)
                gate(1, HC * b + 1, hid_done, 1, sil_rdy, gate_rdy)
                if not last:
                    norm(b + 1)
                dve.wait_ge(nb_done, 4 * b + 1)
                dve.tensor_scalar(rn[:, :, :].rearrange("p t h -> p (t h)"), bank[6][:, 0:64], EPS_N, None, ALU.max).then_inc(kstep, 1)
                dve.wait_ge(kstep, 3 * b + 3)
                dve.reciprocal(rn[:, :, :], rn[:, :, :]).then_inc(rn_rdy, 1)
                gate(2, HC * b + 2, hid_done, 4, sil_rdy, gate_rdy)
                if not last:
                    normalise(b + 1)
                table_rows(b)
                ranks_in(b)
                dve.wait_ge(rhi_rdy, b + 1)
                dve.tensor_tensor(r16_lo, bank[7][0:16, :], r16_hi.bitcast(f32), ALU.subtract).then_inc(rlo_rdy, 1)
                if last:
                    ranks(b)
                    tile_list()
                dve.wait_ge(mhi_rdy, b + 1)
                mflat = "p c n -> p (c n)"
                dve.tensor_tensor(m_lo[:, :, :].rearrange(mflat), bank[4][:, :], m_hi[:, :, :].rearrange(mflat).bitcast(f32),
                                  ALU.subtract).then_inc(mlo_rdy, 1)
                gate(3, HC * b + 3, hid_done, 1, sil_rdy, gate_rdy)
                if not last:
                    ranks(b)
                for c in range(DC):
                    dve.wait_ge(nb_done, 4 * b + 3 + c)
                    dve.tensor_tensor(qn[:, c, :], phiq[:, c, :], bank[6 + c][:, :], ALU.mult).then_inc(qn_rdy, 1)
                for c in range(DC):
                    dve.wait_ge(qhi_rdy, DC * b + c + 1)
                    dve.tensor_tensor(qn_lo[:, c, :], qn[:, c, :], qn_hi[:, c, :].bitcast(f32), ALU.subtract).then_inc(qlo_rdy, 1)
                if not last:
                    t_low(b + 1)
                else:
                    dve.wait_ge(info_done, 1)
                    dve.tensor_copy(info_i[:, :, :].rearrange("p n t -> p (n t)"), bank[2][0:1, 0:3 * NT]).then_inc(infoi_rdy, 1)
                dve.wait_ge(res_rdy, b + 1)
                for n in range(2):
                    dve.wait_ge(y_done, DC * b + n + 1)
                    part_ = res[:, 2 * n:2 * n + 2, :].rearrange("p t d -> p (t d)")
                    dve.tensor_tensor(part_, part_, bank[5 + n][:, :], ALU.add).then_inc(base_rdy, 1)

            def tile_list():
                dve.wait_ge(x_ld, 16 * (B + 1))
                dve.wait_ge(v_link, LN_LINKS + PER * (B - 1) + RT_LINKS + RK_LINKS)

                def step(ins, k):
                    ins.then_inc(t_link, 1)
                    dve.wait_ge(t_link, k)
                step(dve.tensor_tensor(cnt[:, :], run[:, :], slot_row, ALU.subtract), 1)
                step(dve.tensor_scalar(cnt[:, :], cnt[:, :], float(P - 1), None, ALU.add), 2)
                step(dve.tensor_copy(cnt_i[:, :], cnt[:, :]), 3)
                step(dve.tensor_single_scalar(cnt_i[:, :], cnt_i[:, :], 7, ALU.arith_shift_right), 4)
                step(dve.tensor_copy(cnt[:, :], cnt_i[:, :]), 5)
                big = kb[:, :, :].rearrange("p t n -> p (t n)").rearrange("p (a c) -> p a c", a=NSLOT)
                step(dve.tensor_tensor(big, before,
                                       cnt[:, :].unsqueeze(1).broadcast_to([P, NSLOT, NSLOT]), ALU.mult), 6)
                step(dve.tensor_reduce(first[:, :], big, AX, ALU.add), 7)
                step(dve.tensor_tensor(cnt[:, :], cnt[:, :], first[:, :], ALU.add), 8)
                step(dve.tensor_scalar(memb[:, :], first[:, :], part, None, ALU.is_le), 9)
                step(dve.tensor_scalar(cnt[:, :], cnt[:, :], part, None, ALU.is_gt), 10)
                step(dve.tensor_tensor(memb[:, :], memb[:, :], cnt[:, :], ALU.mult), 11)
                step(dve.tensor_tensor(memt[:, 0, :], memb[:, :], slot_ea, ALU.mult), 12)
                step(dve.tensor_tensor(memt[:, 1, :], memb[:, :], slot_eb, ALU.mult), 13)
                step(dve.tensor_scalar(first[:, :], first[:, :], -float(P), part128, ALU.mult, ALU.add), 14)
                step(dve.tensor_tensor(first[:, :], first[:, :], slot_row, ALU.add), 15)
                step(dve.tensor_scalar(first[:, :], first[:, :], -float(SENT), None, ALU.add), 16)
                step(dve.tensor_tensor(memt[:, 2, :], memb[:, :], first[:, :], ALU.mult), 17)
                step(dve.tensor_reduce(info[:, 0:3], memt, AX, ALU.add), 18)
                dve.tensor_scalar(info[:, 2:3], info[:, 2:3], float(SENT), None, ALU.add).then_inc(info_rdy, 1)

            dve.wait_ge(setup_ld, 16 * (14 + len(stage)))
            dve.memset(onec[:, :], 1.0)
            dve.tensor_scalar(nbq[:, :], bq[:, :], -1.0, None, ALU.mult)
            dve.memset(triones[:, 1, :], 1.0)
            dve.tensor_copy(triones[:, 0, :], tri_f)
            dve.tensor_copy(spread[:, :, :], spread_f)
            dve.tensor_copy(run[:, :], slot_row)
            dve.tensor_copy(tok[:, :], tok0).then_inc(const_set, 1)
            dve.wait_ge(const_set, 3)
            dve.tensor_copy(wrt[:, :, 0, :], wrt_f).then_inc(kstep0, 1)
            dve.wait_ge(kstep0, 1)
            dve.tensor_tensor(wrt[:, :, 1, :], wrt_f, wrt[:, :, 0, :].bitcast(f32), ALU.subtract).then_inc(kstep0, 1)
            start(0)
            norm(0)
            normalise(0)
            for n, (buf, _, hi, lo, flat) in enumerate(stage):
                dve.wait_ge(w_round, n + 1)
                h = (hi[:].rearrange(flat) if flat else hi).bitcast(f32)
                ins = dve.tensor_tensor(lo[:].rearrange(flat) if flat else lo, buf, h, ALU.subtract)
                if n == 1:
                    dve.wait_ge(thi, DC)
                    t_low(0)
            ins.then_inc(w_split, 1)
            rounds(dve, batch, B)

            def st_low(g):
                for c in range(DC):
                    dve.wait_ge(sthi, DC * g + c + 1)
                    dve.tensor_tensor(xnT_lo[:, c, :], bank[1 + c][:, :], xnT_hi[:, c, :].bitcast(f32), ALU.subtract).then_inc(stlo, 1)

            def group(g, last):
                ups = (1, 3, 5, 0)
                for j in range(HC):
                    gate(j, HC * g + j, shid_done, ups[j], ssil, sgate)
                    dve.wait_ge(shhi, HC * g + j + 1)
                    dve.tensor_tensor(h_lo[:, j, :], gated[:, j % 2, :], h_hi[:, j, :].bitcast(f32), ALU.subtract).then_inc(shlo, 1)
                if not last:
                    st_low(g + 1)
                dve.wait_ge(bs_ld, 16 * TB * (g + 1))
                dve.wait_ge(cur_rdy, g + 1)
                wts = cur[:, :, :].bitcast(f32)
                for t in range(TB):
                    dve.wait_ge(sw_done, TB * g + t + 1)
                    dve.scalar_tensor_tensor(res[:, t, :], bank[3 + t][:, 0:D], wts[:, t, 1:2], res[:, t, :],
                                             ALU.mult, ALU.add).then_inc(ystep, 1)
                for t in range(TB):
                    dve.wait_ge(ystep, TB * g + t + 1)
                    dve.scalar_tensor_tensor(res[:, t, :], bank[3 + t][:, D:2 * D], wts[:, t, 2:3], res[:, t, :],
                                             ALU.mult, ALU.add).then_inc(ysum, 1)

            st_low(0)
            rounds(dve, group, NG)

        @block.gpsimd
        def _(pool):
            pool.memset(fill[:, :, 1:4], 0).then_inc(fill_set, 1)
            pool.memset(fill[:, :, 0:1], N).then_inc(fill_set, 1)
            pool.memset(wexp_lo[:, 0:D].bitcast(f32), 0.0).then_inc(fill_set, 1)
            pool.memset(mhalf[:, :], -0.5).then_inc(const_set, 1)
            pool.memset(rows[:, :, 3:4], 0).then_inc(const_set, 1)
            pool.wait_ge(const_set, 3)

            def reciprocal_root(b):
                pool.wait_ge(var_rdy, b + 1)
                pool.tensor_tensor(rstd[:, :], var[:, :], mhalf[:, :], ALU.pow).then_inc(rstd_rdy, 1)

            def low(j, n, hhi, hlo):
                pool.wait_ge(hhi, n + 1)
                pool.tensor_tensor(h_lo[:, j, :], gated[:, j % 2, :], h_hi[:, j, :].bitcast(f32), ALU.subtract).then_inc(hlo, 1)

            def batch(b, last):
                wait(pool, base_st, 16 * b)
                pool.wait_ge(x_ld, 16 * (b + 1))
                pool.wait_ge(setup_ld, 16 * (14 + len(stage)))
                pool.tensor_tensor(res[:, :, :], xt[:, :, :], bo[:, :].unsqueeze(1).broadcast_to([P, TB, D]), ALU.add).then_inc(res_rdy, 1)
                low(0, HC * b, hhi_rdy, hlo_rdy)
                low(1, HC * b + 1, hhi_rdy, hlo_rdy)
                if not last:
                    reciprocal_root(b + 1)
                low(2, HC * b + 2, hhi_rdy, hlo_rdy)
                low(3, HC * b + 3, hhi_rdy, hlo_rdy)
                wait_apart(pool, row_rdy, b + 1)
                for t in range(TB):
                    pool.indirect_dma_start(tab_d, bass.IndirectOffsetOnAxis(ap=pos_i[:, t:t + 1], axis=0),
                                            rows[:, t, :], None).then_inc(row_st, 16)
                wait_apart(pool, w_ld, 16 * (b + 1))
                pool.tensor_copy(wexp_hi[:, bass.ds(b * UNIT, UNIT)], wstage[:, :]).then_inc(g_link, 1)
                pool.wait_ge(g_link, b + 1)
                pool.tensor_tensor(wexp_lo[:, bass.ds(b * UNIT, UNIT)], wstage[:, :],
                                   wexp_hi[:, bass.ds(b * UNIT, UNIT)].bitcast(f32), ALU.subtract).then_inc(wexp_split, 1)

            reciprocal_root(0)
            pool.wait_ge(fill_st, 16 * (NCLS + 3))
            rounds(pool, batch, B)

            def gather(d, to, idx, done):
                for t in range(TB):
                    pool.indirect_dma_start(to[:, t, :], None, d, bass.IndirectOffsetOnAxis(ap=idx[:, t:t + 1], axis=0)).then_inc(done, 16)

            def tokens(g):
                wait(pool, xs_ld, 16 * TB * g)
                wait_apart(pool, tab_ld, 16 * TB * (g + 1))
                pool.tensor_copy(idx_next[:, :], tab[:, bass.ds(g * TB, TB), 0]).then_inc(idxn_rdy, 1)
                wait_apart(pool, idxn_rdy, g + 1)
                wait_apart(pool, st_done, DC * g)
                gather(xn_d, xn, idx_next, xs_ld)

            def scatter(g):
                for t in range(TB):
                    wait_apart(pool, ysum, TB * g + t + 1)
                    pool.indirect_dma_start(out, bass.IndirectOffsetOnAxis(ap=idx_cur[:, t:t + 1], axis=0), res[:, t, :], None,
                                            bounds_check=N - 1, oob_is_err=False).then_inc(out_st, 16)

            def bases(g):
                wait_apart(pool, out_st, 16 * TB * g)
                pool.tensor_copy(cur[:, :, :], tab[:, bass.ds(g * TB, TB), :]).then_inc(cur_rdy, 1)
                wait_apart(pool, cur_rdy, g + 1)
                pool.tensor_copy(idx_cur[:, :], cur[:, :, 0]).then_inc(idxc_rdy, 1)
                wait_apart(pool, idxc_rdy, g + 1)
                gather(base_d, res, idx_cur, bs_ld)

            pool.wait_ge(xn_st, 16 * B)
            pool.wait_ge(t_done, DC * B)
            tokens(0)
            pool.wait_ge(base_st, 16 * B)

            def group(g, last):
                if not last:
                    tokens(g + 1)
                if not isinstance(g, int) or g:
                    scatter(g - 1)
                bases(g)

            rounds(pool, group, NG)
            scatter(NG - 1)
            pool.wait_ge(out_st, 16 * TB * NG)


def constants():
    P, D, N = 128, 256, 8192
    p = np.arange(P)
    ident = np.eye(P, dtype=np.float32)
    tri = (p[:, None] < p[None, :]).astype(np.float32)
    head = (p[:, None] // 16 == p[None, :] // 16).astype(np.float32)
    f = (np.arange(2)[None, :, None] * P + p[:, None, None]) // 16
    heads = (f == np.arange(16)[None, None, :]).astype(np.float32)
    spread = np.ascontiguousarray(heads.transpose(2, 1, 0))
    pairs = [(g, j, i) for g in range(2) for j in range(4) for i in range(4) if j < i]
    mask = np.zeros((4, 4), np.float32)
    row, ea, eb = (np.zeros(32, np.float32) for _ in range(3))
    for n, (g, j, i) in enumerate(pairs):
        mask[j, i] = 1
        slot = 16 * g + 4 * j + i
        row[slot], ea[slot], eb[slot] = n * N, (4 * g + j) * 4 * D, (4 * g + i) * 4 * D
    s = np.arange(32)
    before = (s[None, :] < s[:, None]).astype(np.float32)
    before = np.ascontiguousarray(np.broadcast_to(before, (P, 32, 32)))
    crow = np.concatenate([mask.ravel(), row, ea, eb])
    crow = np.ascontiguousarray(np.broadcast_to(crow, (P, crow.size)))
    part = np.stack([p * P, p] + [t * P + p for t in range(4)], 1).astype(np.float32)
    return {"c_ident": ident, "c_tri": tri, "c_head": head, "c_heads": heads, "c_spread": spread,
            "c_row": crow, "c_before": before, "c_part": part}


def kernel(**inputs):
    import concourse.bacc as bacc
    from concourse.bass_utils import run_bass_kernel_spmd

    a = {k: np.asarray(v) for k, v in inputs.items()}

    def chunks(w):
        k, n = w.shape
        return np.ascontiguousarray(w.reshape(k // 128, 128, n).transpose(1, 0, 2))

    def every(b):
        return np.ascontiguousarray(np.broadcast_to(b, (128, b.size)))

    w1 = chunks(a["L0_ffn_w1"].T).reshape(128, -1)
    w2 = np.ascontiguousarray(a["L0_ffn_w2"].transpose(0, 2, 1).reshape(8, 4, 128, 256).transpose(2, 0, 1, 3)).reshape(128, -1)
    arrays = {
        "x": a["L0_attn_inputs_q"],
        "w_kv": chunks(np.concatenate([a["L0_attn_Wk"], a["L0_attn_Wv"]], 1)),
        "w_q": chunks(a["L0_attn_Wq"]),
        "w_o": chunks(a["L0_attn_Wo"]),
        "w_in": chunks(a["L0_ffn_w_in"].T),
        "w_out": chunks(a["L0_ffn_w_out"].T),
        "w_exp": np.concatenate([w1, w2], 1),
        "w_rt": chunks(np.concatenate([a["L0_ffn_wg"], a["L0_ffn_we"]], 0).T),
        "b_q": np.ascontiguousarray(a["L0_attn_bq"].reshape(2, 128).T),
        "b_v": every(a["L0_attn_bv"]),
        "b_k": every(a["L0_attn_bk"]),
        "b_o": every(a["L0_attn_bo"]),
        "b_rt": every(np.concatenate([a["L0_ffn_gb"], a["L0_ffn_eb"]])),
        **constants(),
    }
    arrays = {k: np.ascontiguousarray(v) for k, v in arrays.items()}
    nc = bacc.Bacc("TRN2", target_bir_lowering=False, num_devices=1)
    args = [nc.dram_tensor(k, v.shape, mybir.dt.from_np(v.dtype), kind="ExternalInput").ap() for k, v in arrays.items()]
    args.append(nc.dram_tensor("out", (8192, 256), mybir.dt.float32, kind="ExternalOutput").ap())
    layer_program(nc, *args)
    got = run_bass_kernel_spmd(nc, [arrays], core_ids=[0]).results[0]["out"]
    return got.reshape(16, 512, 256)
```

```python
import numpy as np
import concourse.bass as bass
from concourse import mybir
from contextlib import ExitStack


def layer_program(nc, x, w_k, w_v, w_q, w_o, w_in, w_out, w_exp, w_rt, b_q, b_kl, b_vo,
                  c_stay, c_round, out):
    f32, f32r, bf16, i32 = mybir.dt.float32, mybir.dt.float32r, mybir.dt.bfloat16, mybir.dt.int32
    ALU = mybir.AluOpType
    ACT = mybir.ActivationFunctionType
    AX = mybir.AxisListType.X

    P = 128
    B, S, D = 16, 512, 256
    N = B * S
    TB = S // P
    DC = D // P
    HC = 4
    E = 8
    NCLS = 12
    NSLOT = 32
    TILES = (N + NCLS * (P - 1)) // P
    NG = (TILES + TB - 1) // TB
    NT = NG * TB
    LAST_TILES = TILES - (NG - 1) * TB
    SENT = NCLS * N
    ROWS = SENT + P
    UNIT = (2 * 1024 + E * HC * D) // B
    EPS_LN, EPS_N = 1e-5, 1e-6

    xn_d = nc.dram_tensor("xn_d", (N + P, D), f32, kind="Internal").ap()
    base_d = nc.dram_tensor("base_d", (N + P, D), f32, kind="Internal").ap()
    tab_d = nc.dram_tensor("tab_d", (ROWS, 4), i32, kind="Internal").ap()

    ctx = ExitStack()
    with ctx:
        def sb(name, shape, dt):
            return ctx.enter_context(nc.sbuf_tensor(name, shape, dt))

        def sem(name):
            return ctx.enter_context(nc.semaphore(name))

        def pair(name, shape):
            return sb(name + "_hi", shape, f32r), sb(name + "_lo", shape, f32r)

        KL = D + 10
        wkv_hi, wkv_lo = pair("wkv", [P, DC, KL + D])
        wq_hi, wq_lo = pair("wq", [P, DC, D])
        win_hi, win_lo = pair("win", [P, DC, 1024])
        wout_hi, wout_lo = pair("wout", [P, HC, D])
        wexp_hi, wexp_lo = pair("wexp", [P, B * UNIT])
        wo = sb("wo", [P, DC, D], f32)
        wstage = sb("wstage", [P, UNIT], f32)

        xt = sb("xt", [P, TB, D], f32)
        res = sb("res", [P, TB, D], f32)
        xn = sb("xn", [P, TB, D], f32)
        xnT_hi, xnT_lo = pair("xnT", [P, DC, S])
        kb = sb("kb", [P, TB, D], f32)
        expt = sb("expt", [P, 2, 512], f32)
        relut = sb("relut", [P, 2, 512], f32)
        phik = sb("phik", [P, TB, D], f32)
        v = sb("v", [P, TB, DC, P + 1], f32)
        qn = kb[:, :, :].rearrange("p t n -> p (t n)").rearrange("p (c s) -> p c s", c=DC)
        phiq = sb("phiq", [P, DC, S], f32)
        qn_hi, qn_lo = pair("qn", [P, DC, S])
        gated = sb("gated", [P, 2, S], f32)
        h_hi, h_lo = pair("h", [P, HC, S])
        m_hi, m_lo = pair("m", [P, DC, D])
        rsplit = qn_hi[0:32, 1, :]

        NROW = 16 + 4 * NSLOT
        stay = sb("stay", [P, 2 * P + DC * 16 + NROW + 6], f32)
        ident = stay[:, 0:P]
        head = stay[:, P:2 * P]
        heads = stay[:, 2 * P:2 * P + DC * 16].rearrange("p (c n) -> p c n", c=DC)
        crow = stay[:, 2 * P + DC * 16:2 * P + DC * 16 + NROW]
        cpart = stay[:, 2 * P + DC * 16 + NROW:]
        triones = sb("triones", [P, 2, P], bf16)
        round_f = relut[:, 0, 0:3 * P]
        tri_f = round_f[:, 0:P]
        wrt_f = relut[:, 1, 384:384 + 10 * DC].rearrange("p (c n) -> p c n", c=DC)
        spread = sb("spread", [32, DC, P], f32r)
        spread_f = round_f[0:32, P:3 * P].rearrange("p (c n) -> p c n", c=DC)
        bq = sb("bq", [P, DC], f32)
        nbq = sb("nbq", [P, DC], f32)
        bkl = sb("bkl", [P, KL], f32)
        bk, brt = bkl[:, 0:D], bkl[:, D:KL]
        bvo = sb("bvo", [P, 2 * D], f32)
        bv, bo = bvo[:, 0:D].rearrange("p (c n) -> p c n", c=DC), bvo[:, D:2 * D]

        stats = sb("stats", [P, TB, 6], f32)
        mv = sb("mv", [P, TB, 2], f32)
        var = sb("var", [P, TB], f32)
        mhalf = sb("mhalf", [P, TB], f32)
        rstd = sb("rstd", [P, TB], f32)
        ksum = sb("ksum", [P, DC], f32)
        khead = sb("khead", [P, DC, 16], f32)
        kvm = relut[:, 0, 0:DC * P].rearrange("p (c n) -> p c n", c=DC)
        kvT = relut[:, 1, 0:DC * P].rearrange("p (c n) -> p c n", c=DC)
        rn = sb("rn", [P, TB, 32], f32)

        lg = sb("lg", [P, TB, 10], f32)
        lmax = sb("lmax", [P, TB, 3], f32)
        ex = sb("ex", [P, TB, 10], f32)
        gg = sb("gg", [P, TB, 2], f32)
        gsum = sb("gsum", [P, TB], f32)
        exs = sb("exs", [P, TB, 2, 4], f32)
        w4 = sb("w4", [P, TB, 4], f32)
        esum = sb("esum", [P, TB], f32)
        cmp = sb("cmp", [P, TB, 4, 4], f32)
        cmq = sb("cmq", [P, TB, 4, 4], f32)
        win = sb("win", [P, TB, 4], f32)
        oh = sb("oh", [P, TB, NSLOT], bf16)
        rank = sb("rank", [P, TB + 1, NSLOT], f32)
        run = sb("run", [P, NSLOT], f32)
        pos = sb("pos", [P, TB], f32)
        pos_i = sb("pos_i", [P, TB], i32)
        tok = sb("tok", [P, TB], f32)
        rows = sb("rows", [P, TB, 4], i32)
        fill = wexp_hi[:, B * UNIT - 4 * N // P:].bitcast(i32).rearrange("p (n w) -> p n w", w=4)
        cnt_i = sb("cnt_i", [P, NSLOT], i32)
        memb = sb("memb", [P, NSLOT], f32)
        memt = relut[:, 1, 256:256 + 3 * NSLOT].rearrange("p (n c) -> p n c", n=3)
        info = sb("info", [P, 4], f32)
        info_i = sb("info_i", [1, 3, NT], i32)
        tab = phik[:, :, :].rearrange("p t d -> p (t d)")[:, 0:4 * NT].bitcast(i32).rearrange("p (n w) -> p n w", w=4)
        idx_next = sb("idx_next", [P, TB], i32)
        cur = sb("cur", [P, TB, 4], i32)
        idx_cur = sb("idx_cur", [P, TB], i32)

        pair_mask = crow[:, 0:16]
        slot_row = crow[:, 16:16 + NSLOT]
        slot_ea = crow[:, 16 + NSLOT:16 + 2 * NSLOT]
        slot_eb = crow[:, 16 + 2 * NSLOT:16 + 3 * NSLOT]
        slot_rel = crow[:, 16 + 3 * NSLOT:16 + 4 * NSLOT]
        sums = relut[:, 1, 352:352 + 4 * NSLOT].rearrange("p (n c) -> p n c", n=2)
        part128 = cpart[:, 0:1]
        part = cpart[:, 1:2]
        tok0 = cpart[:, 2:6]

        bank = [ctx.enter_context(nc.psum_tensor(f"bank{i}", [P, 512], f32)) for i in range(8)]

        kv_w_ld = sem("kv_w_ld")
        q_w_ld = sem("q_w_ld")
        in_w_ld = sem("in_w_ld")
        out_w_ld = sem("out_w_ld")
        x_ld = sem("x_ld")
        w_ld = sem("w_ld")
        xn_st = sem("xn_st")
        base_st = sem("base_st")
        fill_st = sem("fill_st")
        w_round = sem("w_round")
        w_split = sem("w_split")
        ffn_split = sem("ffn_split")
        fill_set = sem("fill_set")
        const_set = sem("const_set")
        pool_set = sem("pool_set")
        passed = sem("passed")
        v_link = sem("v_link")
        g_link = sem("g_link")
        wexp_split = sem("wexp_split")
        t_done = sem("t_done")
        k_done = sem("k_done")
        v_done = sem("v_done")
        q_done = sem("q_done")
        hid_done = sem("hid_done")
        acc_done = sem("acc_done")
        rt_done = sem("rt_done")
        kvt_done = sem("kvt_done")
        nb_done = sem("nb_done")
        m_done = sem("m_done")
        y_done = sem("y_done")
        info_done = sem("info_done")
        thi = sem("thi")
        v_rdy = sem("v_rdy")
        ek_rdy = sem("ek_rdy")
        eq_rdy = sem("eq_rdy")
        ex_rdy = sem("ex_rdy")
        neg_rdy = sem("neg_rdy")
        sil_rdy = sem("sil_rdy")
        hhi_rdy = sem("hhi_rdy")
        rhi_rdy = sem("rhi_rdy")
        qhi_rdy = sem("qhi_rdy")
        mhi_rdy = sem("mhi_rdy")
        kvT_rdy = sem("kvT_rdy")
        xn_rdy = sem("xn_rdy")
        tlo = sem("tlo")
        kb_rdy = sem("kb_rdy")
        phik_rdy = sem("phik_rdy")
        phiq_rdy = sem("phiq_rdy")
        lg_rdy = sem("lg_rdy")
        oh_rdy = sem("oh_rdy")
        gate_rdy = sem("gate_rdy")
        kvm_rdy = sem("kvm_rdy")
        var_rdy = sem("var_rdy")
        rank_rd = sem("rank_rd")
        row_rdy = sem("row_rdy")
        rn_rdy = sem("rn_rdy")
        qn_rdy = sem("qn_rdy")
        qlo_rdy = sem("qlo_rdy")
        mlo_rdy = sem("mlo_rdy")
        base_rdy = sem("base_rdy")
        info_rdy = sem("info_rdy")
        kstep = sem("kstep")
        t_link = sem("t_link")
        ystep = sem("ystep")
        infoi_rdy = sem("infoi_rdy")
        rstd_rdy = sem("rstd_rdy")
        res_rdy = sem("res_rdy")
        hlo_rdy = sem("hlo_rdy")
        row_st = sem("row_st")
        tab_ld = sem("tab_ld")
        xs_ld = sem("xs_ld")
        bs_ld = sem("bs_ld")
        out_st = sem("out_st")
        idxn_rdy = sem("idxn_rdy")
        idxc_rdy = sem("idxc_rdy")
        cur_rdy = sem("cur_rdy")
        st_done = sem("st_done")
        shid_done = sem("shid_done")
        sw_done = sem("sw_done")
        sthi = sem("sthi")
        stlo = sem("stlo")
        ssil = sem("ssil")
        sgate = sem("sgate")
        shhi = sem("shhi")
        shlo = sem("shlo")
        ysum = sem("ysum")

        block = ctx.enter_context(nc.Block())

        def wait(e, s, n):
            if not isinstance(n, int) or n > 0:
                e.wait_ge(s, n)

        def wait_apart(e, s, n):
            wait(e, s, n)
            if not isinstance(n, int):
                e.sem_inc(passed, 1)

        def first_row(b):
            return isinstance(b, int) and b == 0

        def rounds(e, body, n):
            body(0, False)
            with e.Fori(1, n - 1) as i:
                body(i, False)
            body(n - 1, True)

        def flat(buf):
            return buf[:, :, :].rearrange("p t n -> p (t n)")

        def by_chunk(cols, n):
            return cols.rearrange("p (c n) -> p c n", n=n)

        stage_kv = [
            (by_chunk(flat(kb)[:, 0:DC * D], D), w_k, wkv_hi[:, :, 0:D], wkv_lo[:, :, 0:D]),
            (wrt_f, w_rt, wkv_hi[:, :, D:KL], wkv_lo[:, :, D:KL]),
            (by_chunk(flat(kb)[:, DC * D:2 * DC * D], D), w_v, wkv_hi[:, :, KL:KL + D], wkv_lo[:, :, KL:KL + D]),
        ]
        stage_q = [(by_chunk(expt[:, 0, :], D), w_q, wq_hi[:, :, :], wq_lo[:, :, :])]
        stage_in = [
            (flat(res), w_in[:, 0, :], win_hi[:, 0, :], win_lo[:, 0, :]),
            (flat(phiq), w_in[:, 1, :], win_hi[:, 1, :], win_lo[:, 1, :]),
        ]
        stage_out = [(by_chunk(flat(gated), D), w_out, wout_hi[:, :, :], wout_lo[:, :, :])]

        def x_rows(b):
            return x[bass.ds(b, 1), :, :].rearrange("o (t p) d -> p (o t) d", p=P)

        def rows_of(d, b):
            return d[bass.ds(b * S, S), :].rearrange("(t p) d -> p t d", p=P)

        zero_rows = wexp_lo[:, B * UNIT - D:].bitcast(f32)

        def mm3(e, to, w_hi, w_lo, m_hi_, m_lo_, first_, last_, free=False):
            e.matmul(to, w_hi, m_hi_, start=first_, stop=False, skip_group_check=free)
            e.matmul(to, w_hi, m_lo_, start=False, stop=False, skip_group_check=free)
            return e.matmul(to, w_lo, m_hi_, start=False, stop=last_, skip_group_check=free)

        @block.sync
        def _(sp):
            sp.dma_start(xt[:, :, :], x[0, :, :].rearrange("(t p) d -> p t d", p=P)).then_inc(x_ld, 16)

            def loads(done, pairs, stage):
                for to, of in [(buf, of) for buf, of, _, _ in stage] + pairs:
                    sp.dma_start(to, of).then_inc(done, 16)
            loads(kv_w_ld, [(stay[:, :], c_stay)], stage_kv)
            loads(q_w_ld, [(bkl[:, :], b_kl), (bq[:, :], b_q), (round_f, c_round)], stage_q)
            loads(in_w_ld, [], stage_in)
            loads(out_w_ld, [(bvo[:, :], b_vo), (wo[:, :, :], w_o)], stage_out)
            sp.wait_ge(fill_set, 3)
            for c in range(NCLS):
                sp.dma_start(tab_d[c * N:(c + 1) * N, :].rearrange("(p n) w -> p n w", p=P), fill[:, :, :]).then_inc(fill_st, 16)
            sp.dma_start(tab_d[SENT:ROWS, :], fill[:, 0, :]).then_inc(fill_st, 16)
            sp.dma_start(xn_d[N:N + P, :], zero_rows).then_inc(fill_st, 16)
            sp.dma_start(base_d[N:N + P, :], zero_rows).then_inc(fill_st, 16)

            def tables(g, opening):
                wait_apart(sp, tab_ld, 16 * TB * g)
                if opening:
                    sp.wait_ge(infoi_rdy, 1)
                    sp.wait_ge(fill_st, 16 * (NCLS + 3))
                at = [sp.value_load(info_i[0:1, 2, bass.ds(g * TB + t, 1)], min_val=0, max_val=SENT) for t in range(TB)]
                if opening:
                    sp.wait_ge(row_st, 16 * TB * B)
                for t in range(TB):
                    sp.dma_start(tab[:, bass.ds(g * TB + t, 1), :].rearrange("p t w -> p (t w)"),
                                 tab_d[bass.ds(at[t], P), :]).then_inc(tab_ld, 16)

            def load_store(b, last):
                wait(sp, wexp_split, b)
                sp.dma_start(wstage[:, :], w_exp[:, bass.ds(b * UNIT, UNIT)]).then_inc(w_ld, 16)
                if not last:
                    sp.wait_ge(res_rdy, b + 1)
                    sp.wait_ge(xn_rdy, b + 1)
                    sp.dma_start(xt[:, :, :], x_rows(b + 1)).then_inc(x_ld, 16)
                    sp.wait_ge(xn_rdy, b + 2)
                    sp.dma_start(rows_of(xn_d, b + 1), xn[:, :, :]).then_inc(xn_st, 16)
                else:
                    tables(0, True)
                sp.wait_ge(base_rdy, DC * (b + 1))
                sp.dma_start(rows_of(base_d, b), res[:, :, :]).then_inc(base_st, 16)

            sp.wait_ge(xn_rdy, 1)
            sp.dma_start(rows_of(xn_d, 0), xn[:, :, :]).then_inc(xn_st, 16)
            rounds(sp, load_store, B)

            with sp.Fori(1, NG) as g:
                tables(g, False)
            sp.wait_ge(xn_st, 16 * B)
            sp.wait_ge(base_st, 16 * B)

        @block.tensor
        def _(pe):
            def transposes(banks, done, free_sem, free_of, ready, ready_n):
                pe.wait_ge(ready, ready_n)
                for c in range(DC):
                    wait(pe, free_sem[c], free_of[c])
                    for t in range(TB):
                        mm = pe.transpose(bank[banks[c]][:, t * P:(t + 1) * P], xn[:, t, c * P:(c + 1) * P], ident)
                    mm.then_inc(done, 1)

            def hidden(j, banks, frees, w_hi, w_lo, done, n=S, split=None):
                for half in range(2):
                    if half == 0:
                        wait(pe, frees[0][0], frees[0][1])
                    else:
                        wait(pe, frees[1][0], frees[1][1])
                    lo = half * 512 + j * P
                    for c in range(DC):
                        if split and half == 0:
                            pe.wait_ge(split[0], split[1] + c + 1)
                        mm = mm3(pe, bank[banks[half]][:, 0:n], w_hi[:, c, lo:lo + P], w_lo[:, c, lo:lo + P],
                                 xnT_hi[:, c, 0:n], xnT_lo[:, c, 0:n], c == 0, c == DC - 1)
                mm.then_inc(done, 1)

            def batch(b, last):
                for t in range(TB):
                    if t == 0:
                        wait(pe, sil_rdy, HC * b)
                    elif t == 1:
                        wait(pe, gate_rdy, HC * b)
                    x_hi, x_lo = xnT_hi[:, :, t * P:(t + 1) * P], xnT_lo[:, :, t * P:(t + 1) * P]
                    for c in range(DC):
                        if t == 0:
                            pe.wait_ge(tlo, DC * b + c + 1)
                        mm = mm3(pe, bank[t][:, 0:KL], x_hi[:, c, :], x_lo[:, c, :],
                                 wkv_hi[:, c, 0:KL], wkv_lo[:, c, 0:KL], c == 0, c == DC - 1)
                    mm.then_inc(k_done, 1)
                    if t == 0:
                        wait(pe, qn_rdy, DC * b)
                    elif t == 2:
                        pe.wait_ge(kb_rdy, TB * b + 1)
                    for c in range(DC):
                        mm = mm3(pe, bank[7 if t < 2 else 0][:, (t % 2) * D:(t % 2 + 1) * D], x_hi[:, c, :], x_lo[:, c, :],
                                 wkv_hi[:, c, KL:KL + D], wkv_lo[:, c, KL:KL + D], t % 2 == 0 and c == 0, c == DC - 1, True)
                    if t % 2 == 1:
                        mm.then_inc(v_done, 1)
                if first_row(b):
                    pe.wait_ge(w_split, 2)
                for o in range(DC):
                    if o == 0:
                        wait(pe, mlo_rdy, b)
                    else:
                        wait(pe, base_rdy, DC * b - 1)
                    for c in range(DC):
                        mm = mm3(pe, bank[4 + o][:, :], wq_hi[:, c, o * P:(o + 1) * P], wq_lo[:, c, o * P:(o + 1) * P],
                                 xnT_hi[:, c, :], xnT_lo[:, c, :], c == 0, c == DC - 1)
                    mm.then_inc(q_done, 1)
                if first_row(b):
                    pe.wait_ge(ffn_split, 2)
                    pe.wait_ge(const_set, 1)
                hidden(0, (6, 7), ((base_rdy, DC * b), (v_rdy, 2 * b + 1)), win_hi, win_lo, hid_done)
                pe.wait_ge(phik_rdy, 2 * (b + 1))
                pe.wait_ge(v_rdy, 2 * (b + 1))
                for c in range(DC):
                    for t in range(TB):
                        mm = pe.matmul(bank[2][:, c * (P + 1):(c + 1) * (P + 1)], phik[:, t, c * P:(c + 1) * P], v[:, t, c, :],
                                       start=(c == 0 and t == 0), stop=(t == TB - 1), skip_group_check=True)
                mm.then_inc(acc_done, 1)
                pe.wait_ge(oh_rdy, b + 1)
                pe.wait_ge(eq_rdy, DC * (b + 1))
                W = NSLOT
                pe.matmul(bank[5][:, 256:256 + TB * W], triones[:, 0, :], oh[:, :, :].rearrange("p t c -> p (t c)"),
                          start=True, stop=False, skip_group_check=True)
                for n in range(TB, 0, -1):
                    o = 256 + (TB + 1 - n) * W
                    mm = pe.matmul(bank[5][:, o:o + n * W], triones[:, 1, :], oh[:, 0:n, :].rearrange("p t c -> p (t c)"),
                                   start=False, stop=(n == 1), skip_group_check=True)
                mm.then_inc(rt_done, 1)
                hidden(1, (0, 1), ((v_rdy, 2 * (b + 1)), (kb_rdy, TB * b + 2)), win_hi, win_lo, hid_done)
                hidden(2, (3, 4), ((kb_rdy, TB * (b + 1)), (eq_rdy, DC * b + 1)), win_hi, win_lo, hid_done)
                pe.wait_ge(phiq_rdy, DC * (b + 1))
                pe.wait_ge(kstep, 6 * b + 2)
                pe.wait_ge(gate_rdy, HC * b + 1)
                for t in range(TB):
                    for c in range(DC):
                        mm = pe.matmul(bank[6][:, 16 * t:16 * t + 16], phiq[:, c, t * P:(t + 1) * P], khead[:, c, :],
                                       start=(c == 0), stop=(c == DC - 1))
                mm.then_inc(nb_done, 1)
                pe.wait_ge(kvm_rdy, b + 1)
                for c in range(DC):
                    mm = pe.transpose(bank[2][:, c * P:(c + 1) * P], kvm[:, c, :], ident)
                mm.then_inc(kvt_done, 1)
                hidden(3, (0, 1), ((sil_rdy, HC * b + 2), (gate_rdy, HC * b + 2)), win_hi, win_lo, hid_done)
                if last:
                    pe.wait_ge(info_rdy, 1)
                    pe.wait_ge(kvT_rdy, B)
                    for n in range(3):
                        mm = pe.matmul(bank[2][0:1, n * NT:(n + 1) * NT], info[0:NT, n:n + 1], ident[0:NT, 0:NT],
                                       start=True, stop=True)
                    mm.then_inc(info_done, 1)
                pe.wait_ge(rn_rdy, b + 1)
                for t in range(TB):
                    mm = pe.transpose(bank[7][0:32, t * P:(t + 1) * P], rn[:, t, :], ident)
                mm.then_inc(nb_done, 1)
                if first_row(b):
                    pe.wait_ge(out_w_ld, 16 * 3)
                    pe.wait_ge(ffn_split, 3)
                pe.wait_ge(kvT_rdy, b + 1)
                pe.wait_ge(gate_rdy, HC * b + 3)
                for c in range(DC):
                    mm = pe.matmul(bank[4][:, c * D:(c + 1) * D], kvT[:, c, :], wo[:, c, :], start=True, stop=True)
                mm.then_inc(m_done, 1)
                if not last:
                    transposes((2, 3), t_done, (kvT_rdy, sil_rdy), (b + 1, HC * b + 3), xn_rdy, b + 2)
                pe.wait_ge(rhi_rdy, b + 1)
                for c in range(DC):
                    mm = pe.matmul(bank[6 + c][:, :], spread[:, c, :], rsplit, start=True, stop=True)
                    mm.then_inc(nb_done, 1)

                def y(t):
                    return bank[5 + t // 2][:, (t % 2) * D:(t % 2 + 1) * D]
                pe.wait_ge(rank_rd, b + 1)
                pe.wait_ge(hlo_rdy, HC * b + 3)
                for t in range(TB):
                    if t == 2:
                        pe.wait_ge(qn_rdy, DC * b + 1)
                    for j in range(HC - 1):
                        mm3(pe, y(t), h_hi[:, j, t * P:(t + 1) * P], h_lo[:, j, t * P:(t + 1) * P],
                            wout_hi[:, j, :], wout_lo[:, j, :], t % 2 == 0 and j == 0, False, True)
                pe.wait_ge(mlo_rdy, b + 1)
                pe.wait_ge(qlo_rdy, DC * (b + 1))
                for t in range(TB):
                    for c in range(DC):
                        mm3(pe, y(t), qn_hi[:, c, t * P:(t + 1) * P], qn_lo[:, c, t * P:(t + 1) * P],
                            m_hi[:, c, :], m_lo[:, c, :], False, False, True)
                pe.wait_ge(hlo_rdy, HC * (b + 1))
                for t in range(TB):
                    mm = mm3(pe, y(t), h_hi[:, 3, t * P:(t + 1) * P], h_lo[:, 3, t * P:(t + 1) * P],
                             wout_hi[:, 3, :], wout_lo[:, 3, :], False, True, True)
                    if t % 2 == 1:
                        mm.then_inc(y_done, 1)

            pe.wait_ge(kv_w_ld, 16 * 4)
            transposes((2, 3), t_done, (t_done, t_done), (0, 0), xn_rdy, 1)
            pe.wait_ge(w_split, 1)
            rounds(pe, batch, B)

            w1_hi = wexp_hi[:, 0:2048].rearrange("p (c n) -> p c n", c=DC)
            w1_lo = wexp_lo[:, 0:2048].rearrange("p (c n) -> p c n", c=DC)
            pe.wait_ge(wexp_split, B)
            pe.wait_ge(infoi_rdy, 1)
            pe.wait_ge(tlo, DC * B)
            transposes((1, 2), st_done, (gate_rdy, infoi_rdy), (HC * B, 1), xs_ld, 16 * TB)

            def group(g, last):
                tiles = LAST_TILES if last else TB

                def experts(t):
                    return [pe.value_load(info_i[0:1, n, bass.ds(g * TB + t, 1)], min_val=0, max_val=(E - 1) * HC * D)
                            for n in range(2)]
                hidden(0, (0, 1), ((sgate, HC * g), (stlo, DC * g + 1)), w1_hi, w1_lo, shid_done, n=tiles * P, split=(stlo, DC * g))
                at = [experts(0)]
                hidden(1, (2, 3), ((stlo, DC * (g + 1)), (ysum, TB * g - 3)), w1_hi, w1_lo, shid_done, n=tiles * P)
                at.append(experts(1))
                if isinstance(g, int) and g == 0:
                    pe.wait_ge(base_rdy, DC * B)
                hidden(2, (4, 5), ((ysum, TB * g - 2), (ysum, TB * g - 1)), w1_hi, w1_lo, shid_done, n=tiles * P)
                at.append(experts(2))
                hidden(3, (6, 0), ((ysum, TB * g), (ssil, HC * g + 1)), w1_hi, w1_lo, shid_done, n=tiles * P)
                at.append(experts(3) if tiles == TB else None)
                if not last:
                    transposes((1, 2), st_done, (sgate, ssil), (HC * g + 1, HC * g + 2), xs_ld, 16 * TB * (g + 2))
                free = ((sgate, HC * g + 2), (ssil, HC * g + 3), (sgate, HC * g + 3), (ssil, HC * g + 4))

                def second(t, js, start, stop):
                    for n in range(2):
                        for j in js:
                            off = at[t][n] + (2048 + j * D)
                            r_hi = wexp_hi[:, bass.ds(off, D)]
                            r_lo = wexp_lo[:, bass.ds(off, D)]
                            mm = mm3(pe, bank[3 + t][:, n * D:(n + 1) * D], h_hi[:, j, t * P:(t + 1) * P],
                                     h_lo[:, j, t * P:(t + 1) * P], r_hi, r_lo, start and n == 0 and j == 0, stop, True)
                    return mm
                pe.wait_ge(shlo, HC * g + 3)
                for t in range(tiles):
                    pe.wait_ge(*free[t])
                    second(t, range(HC - 1), True, False)
                pe.wait_ge(shlo, HC * (g + 1))
                for t in range(tiles):
                    second(t, (HC - 1,), False, True).then_inc(sw_done, 1)

            rounds(pe, group, NG)

        @block.scalar
        def _(act):
            def high_parts(stage):
                for buf, _, hi, _ in stage:
                    act.copy(hi, buf).then_inc(w_round, 1)

            def t_high(b):
                for c in range(DC):
                    act.wait_ge(t_done, DC * b + c + 1)
                    wait(act, hid_done, HC * b)
                    act.copy(xnT_hi[:, c, :], bank[2 + c][:, :]).then_inc(thi, 1)

            def silu(j, n, hid, gate_bank, lo_prev, sil, cols=S):
                act.wait_ge(hid, n + 1)
                wait(act, lo_prev, n - 1)
                act.activation(gated[:, j % 2, 0:cols], bank[gate_bank][:, 0:cols], ACT.Silu).then_inc(sil, 1)

            def high(j, n, gate, hhi, cols=S):
                act.wait_ge(gate, n + 1)
                act.copy(h_hi[:, j, 0:cols], gated[:, j % 2, 0:cols]).then_inc(hhi, 1)

            def batch(b, last):
                if first_row(b):
                    act.wait_ge(w_split, 2)
                    act.wait_ge(const_set, 1)
                for i in range(2):
                    act.wait_ge(v_done, 2 * b + i + 1)
                    wait(act, acc_done, b)
                    act.copy(v[:, 2 * i:2 * i + 2, :, 0:P],
                             bank[7 if i == 0 else 0][:, :].rearrange("p (t c n) -> p t c n", t=2, c=DC)).then_inc(v_rdy, 1)
                    act.wait_ge(kb_rdy, TB * b + 2 * i + 2)
                    wait(act, phiq_rdy, DC * (b - 1) + i + 1)
                    src = kb[:, 2 * i:2 * i + 2, :].rearrange("p t n -> p (t n)")
                    act.activation(expt[:, i, :], src, ACT.Relu, scale=-1.0).then_inc(neg_rdy, 1)
                    act.wait_ge(neg_rdy, 4 * b + i + 1)
                    act.activation(expt[:, i, :], expt[:, i, :], ACT.Exp, scale=-1.0).then_inc(ek_rdy, 1)
                act.wait_ge(lg_rdy, b + 1)
                act.activation(ex[:, :, :], lg[:, :, :], ACT.Exp).then_inc(ex_rdy, 1)
                for o in range(DC):
                    act.wait_ge(q_done, DC * b + o + 1)
                    act.wait_ge(phik_rdy, 2 * b + o + 1)
                    act.activation(expt[:, o, :], bank[4 + o][:, :], ACT.Relu, bias=nbq[:, o:o + 1], scale=-1.0).then_inc(neg_rdy, 1)
                    act.activation(relut[:, o, :], bank[4 + o][:, :], ACT.Relu, bias=bq[:, o:o + 1])
                    act.wait_ge(neg_rdy, 4 * b + o + 3)
                    act.activation(expt[:, o, :], expt[:, o, :], ACT.Exp, scale=-1.0).then_inc(eq_rdy, 1)
                wait(act, y_done, DC * b)
                gates = (6, 0, 3, 0)
                if first_row(b):
                    act.wait_ge(ffn_split, 3)
                for j in range(HC):
                    silu(j, HC * b + j, hid_done, gates[j], hlo_rdy, sil_rdy)
                    if j == 3:
                        act.wait_ge(nb_done, 4 * b + 2)
                        act.copy(rsplit, bank[7][0:32, :]).then_inc(rhi_rdy, 1)
                        act.wait_ge(m_done, b + 1)
                        act.copy(m_hi[:, :, :].rearrange("p c n -> p (c n)"), bank[4][:, :]).then_inc(mhi_rdy, 1)
                    if j == 2:
                        act.wait_ge(kvt_done, b + 1)
                        act.copy(kvT[:, :, :].rearrange("p c n -> p (c n)"), bank[2][:, 0:DC * P]).then_inc(kvT_rdy, 1)
                    high(j, HC * b + j, gate_rdy, hhi_rdy)
                for c in range(DC):
                    act.wait_ge(qn_rdy, DC * b + c + 1)
                    act.copy(qn_hi[:, c, :], qn[:, c, :]).then_inc(qhi_rdy, 1)
                if not last:
                    t_high(b + 1)

            act.wait_ge(kv_w_ld, 16 * 4)
            high_parts(stage_kv)
            act.wait_ge(q_w_ld, 16 * 4)
            high_parts(stage_q)
            t_high(0)
            act.wait_ge(in_w_ld, 16 * 2)
            high_parts(stage_in)
            rounds(act, batch, B)

            def st_high(g):
                for c in range(DC):
                    act.wait_ge(st_done, DC * g + c + 1)
                    wait(act, shid_done, HC * g)
                    act.copy(xnT_hi[:, c, :], bank[1 + c][:, :]).then_inc(sthi, 1)

            def group(g, last):
                gates = (0, 2, 4, 6)
                cols = (LAST_TILES if last else TB) * P
                wait(act, sw_done, TB * g)
                for j in range(HC):
                    silu(j, HC * g + j, shid_done, gates[j], shlo, ssil, cols)
                    high(j, HC * g + j, sgate, shhi, cols)
                if not last:
                    st_high(g + 1)

            act.wait_ge(hid_done, HC * B)
            act.wait_ge(y_done, DC * B)
            act.wait_ge(hlo_rdy, HC * B)
            st_high(0)
            rounds(act, group, NG)

        @block.vector
        def _(dve):
            LN_LINKS, RT_LINKS = 2, 21
            PER = LN_LINKS + RT_LINKS
            state = [0, 0]

            def start(n):
                state[:] = n, 0

            def link(ins):
                ins.then_inc(v_link, 1)
                state[1] += 1
                dve.wait_ge(v_link, state[0] + state[1])

            def norm(b):
                dve.wait_ge(x_ld, 16 * (b + 1))
                for t in range(TB):
                    ins = dve.bn_stats(stats[:, t, :], xt[:, t, :])
                link(ins)
                if not isinstance(b, int):
                    dve.sem_inc(passed, 1)
                for t in range(TB):
                    ins = dve.bn_aggr(mv[:, t, :], stats[:, t, :])
                link(ins)
                dve.tensor_scalar(var[:, :], mv[:, :, 1], EPS_LN, None, ALU.add).then_inc(var_rdy, 1)

            def normalise(b):
                dve.wait_ge(rstd_rdy, b + 1)
                wait(dve, xn_st, 16 * b)
                wait(dve, t_done, DC * b)
                for t in range(TB):
                    ins = dve.tensor_scalar(xn[:, t, :], xt[:, t, :], mv[:, t, 0:1], rstd[:, t:t + 1], ALU.subtract, ALU.mult)
                ins.then_inc(xn_rdy, 1)

            def t_low(b):
                for c in range(DC):
                    dve.wait_ge(thi, DC * b + c + 1)
                    dve.tensor_tensor(xnT_lo[:, c, :], bank[2 + c][:, :], xnT_hi[:, c, :].bitcast(f32), ALU.subtract).then_inc(tlo, 1)

            def logits_in(b):
                dve.wait_ge(kb_rdy, TB * (b + 1))
                link(dve.tensor_tensor(lmax[:, :, 0], lg[:, :, 0], lg[:, :, 1], ALU.max))
                link(dve.tensor_reduce(lmax[:, :, 1:3], lg[:, :, 2:10].rearrange("p t (g e) -> p t g e", g=2), AX, ALU.max))
                dve.tensor_tensor(lg[:, :, 0:2], lg[:, :, 0:2], lmax[:, :, 0:1].broadcast_to([P, TB, 2]), ALU.subtract)
                l8 = lg[:, :, 2:10].rearrange("p t (g e) -> p t g e", g=2)
                dve.tensor_tensor(l8, l8, lmax[:, :, 1:3].unsqueeze(3).broadcast_to([P, TB, 2, 4]), ALU.subtract).then_inc(lg_rdy, 1)

            wj = w4[:, :, :].unsqueeze(3).broadcast_to([P, TB, 4, 4])
            wi = w4[:, :, :].unsqueeze(2).broadcast_to([P, TB, 4, 4])

            def probabilities(b):
                dve.wait_ge(ex_rdy, b + 1)
                dve.tensor_tensor(gsum[:, :], ex[:, :, 0], ex[:, :, 1], ALU.add)
                link(dve.tensor_tensor(gg[:, :, 1], ex[:, :, 1], ex[:, :, 0], ALU.is_gt))
                link(dve.tensor_scalar(gg[:, :, 0], gg[:, :, 1], -1.0, 1.0, ALU.mult, ALU.add))
                g4 = gg[:, :, :].unsqueeze(3).broadcast_to([P, TB, 2, 4])
                link(dve.tensor_tensor(exs[:, :, :, :], ex[:, :, 2:10].rearrange("p t (g e) -> p t g e", g=2), g4, ALU.mult))
                link(dve.tensor_tensor(w4[:, :, :], exs[:, :, 0, :], exs[:, :, 1, :], ALU.add))
                link(dve.tensor_reduce(esum[:, :], w4[:, :, :], AX, ALU.add))
                link(dve.tensor_tensor(esum[:, :], esum[:, :], gsum[:, :], ALU.mult))
                link(dve.reciprocal(gsum[:, :], esum[:, :]))
                link(dve.tensor_tensor(w4[:, :, :], w4[:, :, :], gsum[:, :].unsqueeze(2).broadcast_to([P, TB, 4]), ALU.mult))

            def best_two(b):
                msk = pair_mask.rearrange("p (j i) -> p j i", j=4).unsqueeze(1).broadcast_to([P, TB, 4, 4])
                dve.tensor_tensor(cmp[:, :, :, :], wj, wi, ALU.is_gt)
                link(dve.tensor_tensor(cmq[:, :, :, :], wj, wi, ALU.is_equal))
                link(dve.tensor_tensor(cmq[:, :, :, :], cmq[:, :, :, :], msk, ALU.mult))
                link(dve.tensor_tensor(cmp[:, :, :, :], cmp[:, :, :, :], cmq[:, :, :, :], ALU.add))
                link(dve.tensor_reduce(win[:, :, :], cmp[:, :, :, :], AX, ALU.add))
                link(dve.tensor_scalar(win[:, :, :], win[:, :, :], 2.0, None, ALU.is_ge))
                link(dve.tensor_tensor(cmp[:, :, :, :], win[:, :, :].unsqueeze(3).broadcast_to([P, TB, 4, 4]),
                                       win[:, :, :].unsqueeze(2).broadcast_to([P, TB, 4, 4]), ALU.mult))
                link(dve.tensor_tensor(cmp[:, :, :, :], cmp[:, :, :, :], msk, ALU.mult))
                pr = cmp[:, :, :, :].rearrange("p t j i -> p t (j i)")
                for g in range(2):
                    ins = dve.tensor_tensor(oh[:, :, 16 * g:16 * g + 16], pr, gg[:, :, g:g + 1].broadcast_to([P, TB, 16]), ALU.mult)
                ins.then_inc(oh_rdy, 1)

            rank_bank = bank[5][:, 256:256 + 5 * NSLOT].rearrange("p (t c) -> p t c", c=NSLOT)

            def ranks_in(b):
                dve.wait_ge(rt_done, b + 1)
                dve.tensor_tensor(rank[:, :, :], rank_bank, run[:, :].unsqueeze(1).broadcast_to([P, TB + 1, NSLOT]),
                                  ALU.add).then_inc(rank_rd, 1)

            def table_rows(b):
                wait(dve, row_st, 16 * TB * b)
                dve.wait_ge(rank_rd, b + 1)
                wts = rows[:, :, :].bitcast(f32)
                q = cmq[:, :, :, :].rearrange("p t j i -> p t (j i)")
                dve.tensor_copy(run[:, :], rank[:, TB, :])
                link(dve.tensor_tensor(cmq[:, :, :, :], cmp[:, :, :, :], wj, ALU.mult))
                dve.tensor_tensor(rank[:, 0:TB, :], rank[:, 0:TB, :], oh[:, :, :], ALU.mult)
                link(dve.tensor_reduce(wts[:, :, 1], q, AX, ALU.add))
                dve.tensor_reduce(pos[:, :], rank[:, 0:TB, :], AX, ALU.add)
                link(dve.tensor_tensor(cmq[:, :, :, :], cmp[:, :, :, :], wi, ALU.mult))
                dve.tensor_copy(pos_i[:, :], pos[:, :])
                dve.tensor_copy(rows[:, :, 0], tok[:, :])
                link(dve.tensor_reduce(wts[:, :, 2], q, AX, ALU.add))
                dve.tensor_scalar(tok[:, :], tok[:, :], float(S), None, ALU.add).then_inc(row_rdy, 1)

            def gate(j, n, up_bank, sil, out_sem, cols=S):
                dve.wait_ge(sil, n + 1)
                dve.tensor_tensor(gated[:, j % 2, 0:cols], gated[:, j % 2, 0:cols], bank[up_bank][:, 0:cols], ALU.mult).then_inc(out_sem, 1)

            def batch(b, last):
                start(LN_LINKS + PER * b)

                def k_in(t):
                    dve.wait_ge(k_done, TB * b + t + 1)
                    dve.tensor_tensor(kb[:, t, :], bank[t][:, 0:D], bk, ALU.add)
                    dve.tensor_tensor(lg[:, t, :], bank[t][:, D:KL], brt, ALU.add).then_inc(kb_rdy, 1)

                def phi_k(i):
                    dve.wait_ge(ek_rdy, 2 * b + i + 1)
                    wait(dve, acc_done, b)
                    dve.scalar_tensor_tensor(phik[:, 2 * i:2 * i + 2, :].rearrange("p t n -> p (t n)"),
                                             kb[:, 2 * i:2 * i + 2, :].rearrange("p t n -> p (t n)"), 0.0,
                                             expt[:, i, :], ALU.max, ALU.add).then_inc(phik_rdy, 1)

                for t in range(TB):
                    k_in(t)
                phi_k(0)
                logits_in(b)
                phi_k(1)
                probabilities(b)
                wait(dve, rt_done, b)
                best_two(b)
                if first_row(b):
                    dve.wait_ge(ffn_split, 2)
                for o in range(DC):
                    dve.wait_ge(eq_rdy, DC * b + o + 1)
                    wait(dve, nb_done, 4 * (b - 1) + 1)
                    dve.tensor_tensor(phiq[:, o, :], expt[:, o, :], relut[:, o, :], ALU.add).then_inc(phiq_rdy, 1)
                acc = bank[2][:, 0:DC * (P + 1)].rearrange("p (c n) -> p c n", c=DC)
                if first_row(b):
                    dve.wait_ge(out_w_ld, 16 * 3)
                dve.wait_ge(acc_done, b + 1)
                dve.tensor_copy(ksum[:, :], acc[:, :, P]).then_inc(kstep, 1)
                dve.wait_ge(kstep, 6 * b + 1)
                for c in range(DC):
                    ins = dve.tensor_scalar(khead[:, c, :], heads[:, c, :], ksum[:, c:c + 1], None, ALU.mult)
                ins.then_inc(kstep, 1)
                gate(0, HC * b, 7, sil_rdy, gate_rdy)
                for c in range(DC):
                    ins = dve.scalar_tensor_tensor(kvm[:, c, :], bv[:, c, :], ksum[:, c:c + 1], acc[:, c, 0:P],
                                                   ALU.mult, ALU.add)
                ins.then_inc(kstep, 1)
                dve.wait_ge(kstep, 6 * b + 3)
                dve.tensor_tensor(kvm[:, :, :], kvm[:, :, :], head.unsqueeze(1).broadcast_to([P, DC, P]),
                                  ALU.mult).then_inc(kvm_rdy, 1)
                if not last:
                    gate(1, HC * b + 1, 1, sil_rdy, gate_rdy)
                    norm(b + 1)
                else:
                    ranks_in(b)
                    table_rows(b)
                    gate(1, HC * b + 1, 1, sil_rdy, gate_rdy)
                    tile_list()
                dve.wait_ge(nb_done, 4 * b + 1)
                whole, high_part = rn[:, :, 16:32], rn[:, :, 0:16]
                dve.tensor_scalar(whole, bank[6][:, 0:64].rearrange("p (t h) -> p t h", t=TB), EPS_N, None, ALU.max).then_inc(kstep, 1)
                dve.wait_ge(kstep, 6 * b + 4)
                dve.reciprocal(whole, whole).then_inc(kstep, 1)
                dve.wait_ge(kstep, 6 * b + 5)
                dve.tensor_copy(high_part.bitcast(f32r), whole).then_inc(kstep, 1)
                dve.wait_ge(kstep, 6 * b + 6)
                dve.tensor_tensor(whole, whole, high_part, ALU.subtract).then_inc(rn_rdy, 1)
                gate(2, HC * b + 2, 4, sil_rdy, gate_rdy)
                if not last:
                    normalise(b + 1)
                    ranks_in(b)
                else:
                    dve.wait_ge(info_done, 1)
                    dve.tensor_copy(info_i[:, :, :].rearrange("p n t -> p (n t)"), bank[2][0:1, 0:3 * NT]).then_inc(infoi_rdy, 1)
                dve.wait_ge(mhi_rdy, b + 1)
                mflat = "p c n -> p (c n)"
                dve.tensor_tensor(m_lo[:, :, :].rearrange(mflat), bank[4][:, :], m_hi[:, :, :].rearrange(mflat).bitcast(f32),
                                  ALU.subtract).then_inc(mlo_rdy, 1)
                gate(3, HC * b + 3, 1, sil_rdy, gate_rdy)
                for c in range(DC):
                    dve.wait_ge(nb_done, 4 * b + 3 + c)
                    dve.tensor_tensor(qn[:, c, :], phiq[:, c, :], bank[6 + c][:, :], ALU.mult).then_inc(qn_rdy, 1)
                for c in range(DC):
                    dve.wait_ge(qhi_rdy, DC * b + c + 1)
                    dve.tensor_tensor(qn_lo[:, c, :], qn[:, c, :], qn_hi[:, c, :].bitcast(f32), ALU.subtract).then_inc(qlo_rdy, 1)
                if not last:
                    table_rows(b)
                    t_low(b + 1)
                dve.wait_ge(res_rdy, b + 1)
                for n in range(2):
                    dve.wait_ge(y_done, DC * b + n + 1)
                    two = res[:, 2 * n:2 * n + 2, :].rearrange("p t d -> p (t d)")
                    dve.tensor_tensor(two, two, bank[5 + n][:, :], ALU.add).then_inc(base_rdy, 1)

            def tile_list():
                dve.wait_ge(v_link, LN_LINKS + PER * (B - 1) + RT_LINKS)
                steps = [0]

                def step(ins):
                    ins.then_inc(t_link, 1)
                    steps[0] += 1
                    dve.wait_ge(t_link, steps[0])

                step(dve.scalar_tensor_tensor(cnt_i[:, :], run[:, :], float(P - 1), slot_row, ALU.add, ALU.subtract))
                step(dve.tensor_single_scalar(cnt_i[:, :], cnt_i[:, :], 7, ALU.arith_shift_right))
                dve.memset(sums[:, :, 0:NSLOT], 0.0)
                step(dve.tensor_copy(sums[:, 0, NSLOT:], cnt_i[:, :]))
                a, k = 0, 1
                while k < NSLOT:
                    step(dve.tensor_tensor(sums[:, 1 - a, NSLOT:], sums[:, a, NSLOT:],
                                           sums[:, a, NSLOT - k:2 * NSLOT - k], ALU.add))
                    a, k = 1 - a, 2 * k
                first, end = sums[:, a, NSLOT - 1:2 * NSLOT - 1], sums[:, a, NSLOT:]
                step(dve.tensor_scalar(memb[:, :], first, part, None, ALU.is_le))
                step(dve.scalar_tensor_tensor(memb[:, :], end, part, memb[:, :], ALU.is_gt, ALU.mult))
                dve.tensor_tensor(memt[:, 0, :], memb[:, :], slot_ea, ALU.mult)
                dve.tensor_tensor(memt[:, 1, :], memb[:, :], slot_eb, ALU.mult)
                step(dve.scalar_tensor_tensor(memt[:, 2, :], first, -float(P), slot_rel, ALU.mult, ALU.add))
                step(dve.scalar_tensor_tensor(memt[:, 2, :], memt[:, 2, :], part128, memb[:, :], ALU.add, ALU.mult))
                step(dve.tensor_reduce(info[:, 0:3], memt, AX, ALU.add))
                dve.tensor_scalar(info[:, 2:3], info[:, 2:3], float(SENT), None, ALU.add).then_inc(info_rdy, 1)

            def low_parts(stage, n):
                for buf, _, hi, lo in stage:
                    n += 1
                    dve.wait_ge(w_round, n)
                    ins = dve.tensor_tensor(lo, buf, hi.bitcast(f32), ALU.subtract)
                ins.then_inc(w_split, 1)

            dve.memset(triones[:, 1, :], 1.0)
            dve.memset(v[:, :, :, P:P + 1], 1.0)
            start(0)
            norm(0)
            normalise(0)
            low_parts(stage_kv, 0)
            t_low(0)
            low_parts(stage_q, len(stage_kv))
            dve.wait_ge(q_w_ld, 16 * 4)
            dve.wait_ge(kv_w_ld, 16 * 4)
            dve.tensor_scalar(nbq[:, :], bq[:, :], -1.0, None, ALU.mult)
            dve.tensor_copy(triones[:, 0, :], tri_f)
            dve.tensor_copy(spread[:, :, :], spread_f)
            dve.tensor_copy(run[:, :], slot_row)
            dve.tensor_copy(tok[:, :], tok0).then_inc(const_set, 1)
            dve.wait_ge(const_set, 1)
            dve.wait_ge(w_split, 2)
            rounds(dve, batch, B)

            def st_low(g):
                for c in range(DC):
                    dve.wait_ge(sthi, DC * g + c + 1)
                    dve.tensor_tensor(xnT_lo[:, c, :], bank[1 + c][:, :], xnT_hi[:, c, :].bitcast(f32), ALU.subtract).then_inc(stlo, 1)

            def group(g, last):
                ups = (1, 3, 5, 0)
                tiles = LAST_TILES if last else TB
                cols = tiles * P
                for j in range(HC):
                    gate(j, HC * g + j, ups[j], ssil, sgate, cols)
                    dve.wait_ge(shhi, HC * g + j + 1)
                    dve.tensor_tensor(h_lo[:, j, 0:cols], gated[:, j % 2, 0:cols], h_hi[:, j, 0:cols].bitcast(f32), ALU.subtract).then_inc(shlo, 1)
                if not last:
                    st_low(g + 1)
                dve.wait_ge(bs_ld, 16 * TB * (g + 1))
                dve.wait_ge(cur_rdy, g + 1)
                wts = cur[:, :, :].bitcast(f32)

                def add(t, n):
                    dve.wait_ge((sw_done, ystep)[n], TB * g + t + 1)
                    dve.scalar_tensor_tensor(res[:, t, :], bank[3 + t][:, n * D:(n + 1) * D], wts[:, t, n + 1:n + 2], res[:, t, :],
                                             ALU.mult, ALU.add).then_inc((ystep, ysum)[n], 1)
                for t in range(tiles):
                    add(t, 0)
                    if t:
                        add(t - 1, 1)
                add(tiles - 1, 1)

            st_low(0)
            rounds(dve, group, NG)

        @block.gpsimd
        def _(pool):
            pool.memset(fill[:, :, 1:4], 0).then_inc(fill_set, 1)
            pool.memset(fill[:, :, 0:1], N).then_inc(fill_set, 1)
            pool.memset(zero_rows, 0.0).then_inc(fill_set, 1)
            pool.memset(mhalf[:, :], -0.5).then_inc(pool_set, 1)
            pool.memset(rows[:, :, 3:4], 0).then_inc(pool_set, 1)
            pool.wait_ge(pool_set, 2)

            def reciprocal_root(b):
                pool.wait_ge(var_rdy, b + 1)
                pool.tensor_tensor(rstd[:, :], var[:, :], mhalf[:, :], ALU.pow).then_inc(rstd_rdy, 1)

            def low(j, n, hhi, hlo):
                pool.wait_ge(hhi, n + 1)
                pool.tensor_tensor(h_lo[:, j, :], gated[:, j % 2, :], h_hi[:, j, :].bitcast(f32), ALU.subtract).then_inc(hlo, 1)

            def batch(b, last):
                wait(pool, base_st, 16 * b)
                pool.wait_ge(x_ld, 16 * (b + 1))
                pool.tensor_tensor(res[:, :, :], xt[:, :, :], bo.unsqueeze(1).broadcast_to([P, TB, D]), ALU.add).then_inc(res_rdy, 1)
                wait_apart(pool, w_ld, 16 * (b + 1))
                pool.tensor_copy(wexp_hi[:, bass.ds(b * UNIT, UNIT)], wstage[:, :]).then_inc(g_link, 1)
                pool.wait_ge(g_link, b + 1)
                pool.tensor_tensor(wexp_lo[:, bass.ds(b * UNIT, UNIT)], wstage[:, :],
                                   wexp_hi[:, bass.ds(b * UNIT, UNIT)].bitcast(f32), ALU.subtract).then_inc(wexp_split, 1)
                low(0, HC * b, hhi_rdy, hlo_rdy)
                if not last:
                    reciprocal_root(b + 1)
                low(1, HC * b + 1, hhi_rdy, hlo_rdy)

                def table_out():
                    if first_row(b):
                        pool.wait_ge(fill_st, 16 * (NCLS + 3))
                    wait_apart(pool, row_rdy, b + 1)
                    for t in range(TB):
                        pool.indirect_dma_start(tab_d, bass.IndirectOffsetOnAxis(ap=pos_i[:, t:t + 1], axis=0),
                                                rows[:, t, :], None).then_inc(row_st, 16)
                if last:
                    table_out()
                low(2, HC * b + 2, hhi_rdy, hlo_rdy)
                low(3, HC * b + 3, hhi_rdy, hlo_rdy)
                if not last:
                    table_out()

            reciprocal_root(0)
            for n, (buf, _, hi, lo) in enumerate(stage_in):
                pool.wait_ge(w_round, len(stage_kv) + len(stage_q) + n + 1)
                pool.tensor_tensor(lo, buf, hi.bitcast(f32), ALU.subtract).then_inc(ffn_split, 1)
            pool.wait_ge(out_w_ld, 16 * 3)
            for buf, _, hi, lo in stage_out:
                pool.tensor_copy(hi, buf).then_inc(pool_set, 1)
                pool.wait_ge(pool_set, 3)
                pool.tensor_tensor(lo, buf, hi.bitcast(f32), ALU.subtract).then_inc(ffn_split, 1)
            pool.wait_ge(ffn_split, 3)
            rounds(pool, batch, B)

            def gather(d, to, idx, done):
                for t in range(TB):
                    pool.indirect_dma_start(to[:, t, :], None, d, bass.IndirectOffsetOnAxis(ap=idx[:, t:t + 1], axis=0)).then_inc(done, 16)

            def tokens(g):
                wait(pool, xs_ld, 16 * TB * g)
                wait_apart(pool, tab_ld, 16 * TB * (g + 1))
                pool.tensor_copy(idx_next[:, :], tab[:, bass.ds(g * TB, TB), 0]).then_inc(idxn_rdy, 1)
                wait_apart(pool, idxn_rdy, g + 1)
                wait_apart(pool, st_done, DC * g)
                gather(xn_d, xn, idx_next, xs_ld)

            def scatter(g, tiles=TB):
                for t in range(tiles):
                    wait_apart(pool, ysum, TB * g + t + 1)
                    pool.indirect_dma_start(out, bass.IndirectOffsetOnAxis(ap=idx_cur[:, t:t + 1], axis=0), res[:, t, :], None,
                                            bounds_check=N - 1, oob_is_err=False).then_inc(out_st, 16)

            def bases(g):
                wait_apart(pool, out_st, 16 * TB * g)
                pool.tensor_copy(cur[:, :, :], tab[:, bass.ds(g * TB, TB), :]).then_inc(cur_rdy, 1)
                wait_apart(pool, cur_rdy, g + 1)
                pool.tensor_copy(idx_cur[:, :], cur[:, :, 0]).then_inc(idxc_rdy, 1)
                wait_apart(pool, idxc_rdy, g + 1)
                gather(base_d, res, idx_cur, bs_ld)

            pool.wait_ge(xn_st, 16 * B)
            pool.wait_ge(t_done, DC * B)
            tokens(0)
            pool.wait_ge(base_st, 16 * B)

            def group(g, last):
                if not last:
                    tokens(g + 1)
                if not isinstance(g, int) or g:
                    scatter(g - 1)
                bases(g)

            rounds(pool, group, NG)
            scatter(NG - 1, LAST_TILES)
            pool.wait_ge(out_st, 16 * (TB * (NG - 1) + LAST_TILES))


def constants():
    P, D, N = 128, 256, 8192
    p = np.arange(P)
    ident = np.eye(P, dtype=np.float32)
    tri = (p[:, None] < p[None, :]).astype(np.float32)
    head = (p[:, None] // 16 == p[None, :] // 16).astype(np.float32)
    f = (np.arange(2)[None, :, None] * P + p[:, None, None]) // 16
    heads = (f == np.arange(16)[None, None, :]).astype(np.float32)
    spread = np.ascontiguousarray(np.concatenate([heads, heads], 2).transpose(2, 1, 0))
    pairs = [(g, j, i) for g in range(2) for j in range(4) for i in range(4) if j < i]
    mask = np.zeros((4, 4), np.float32)
    row, ea, eb = (np.zeros(32, np.float32) for _ in range(3))
    for n, (g, j, i) in enumerate(pairs):
        mask[j, i] = 1
        slot = 16 * g + 4 * j + i
        row[slot], ea[slot], eb[slot] = n * N, (4 * g + j) * 4 * D, (4 * g + i) * 4 * D
    crow = np.concatenate([mask.ravel(), row, ea, eb, row - 12 * N])
    crow = np.broadcast_to(crow, (P, crow.size))
    part = np.stack([p * P, p] + [t * P + p for t in range(4)], 1)
    stay = np.concatenate([ident, head, heads.reshape(P, -1), crow, part], 1)
    pad = np.zeros((P - 32, 2 * P))
    other = np.concatenate([tri, np.concatenate([spread.reshape(32, -1), pad])], 1)
    return {"c_stay": stay.astype(np.float32), "c_round": other.astype(np.float32)}


def kernel(**inputs):
    import concourse.bacc as bacc
    from concourse.bass_utils import run_bass_kernel_spmd

    a = {k: np.asarray(v) for k, v in inputs.items()}

    def chunks(w):
        k, n = w.shape
        return np.ascontiguousarray(w.reshape(k // 128, 128, n).transpose(1, 0, 2))

    def every(b):
        return np.ascontiguousarray(np.broadcast_to(b, (128, b.size)))

    w1 = chunks(a["L0_ffn_w1"].T).reshape(128, -1)
    w2 = np.ascontiguousarray(a["L0_ffn_w2"].transpose(0, 2, 1).reshape(8, 4, 128, 256).transpose(2, 0, 1, 3)).reshape(128, -1)
    arrays = {
        "x": a["L0_attn_inputs_q"],
        "w_k": chunks(a["L0_attn_Wk"]),
        "w_v": chunks(a["L0_attn_Wv"]),
        "w_q": chunks(a["L0_attn_Wq"]),
        "w_o": chunks(a["L0_attn_Wo"]),
        "w_in": chunks(a["L0_ffn_w_in"].T),
        "w_out": chunks(a["L0_ffn_w_out"].T),
        "w_exp": np.concatenate([w1, w2], 1),
        "w_rt": chunks(np.concatenate([a["L0_ffn_wg"], a["L0_ffn_we"]], 0).T),
        "b_q": np.ascontiguousarray(a["L0_attn_bq"].reshape(2, 128).T),
        "b_kl": every(np.concatenate([a["L0_attn_bk"], a["L0_ffn_gb"], a["L0_ffn_eb"]])),
        "b_vo": every(np.concatenate([a["L0_attn_bv"], a["L0_attn_bo"]])),
        **constants(),
    }
    arrays = {k: np.ascontiguousarray(v) for k, v in arrays.items()}
    nc = bacc.Bacc("TRN2", target_bir_lowering=False, num_devices=1)
    args = [nc.dram_tensor(k, v.shape, mybir.dt.from_np(v.dtype), kind="ExternalInput").ap() for k, v in arrays.items()]
    args.append(nc.dram_tensor("out", (8192, 256), mybir.dt.float32, kind="ExternalOutput").ap())
    layer_program(nc, *args)
    got = run_bass_kernel_spmd(nc, [arrays], core_ids=[0]).results[0]["out"]
    return got.reshape(16, 512, 256)
```
